# Optimizing a Trainium2 kernel written in Bass

```python
import numpy as np
import jax
import jax.numpy as jnp

def _softmax(x, axis=-1):
    return jax.nn.softmax(x, axis=axis)

def _gelu(x):
    return jax.nn.gelu(x, approximate=True)

def _silu(x):
    return jax.nn.silu(x)

def _sigmoid(x):
    return jax.nn.sigmoid(x)

def _layernorm(x, axis=-1, eps=1e-05):
    m = jnp.mean(x, axis=axis, keepdims=True)
    v = jnp.var(x, axis=axis, keepdims=True)
    return (x - m) / jnp.sqrt(v + eps)

def _scatter_add(tgt, idx, src, axis=0):
    return tgt.at[idx].add(src)

def _segment_sum(src, seg, n):
    return jax.ops.segment_sum(src, seg, n)
kernel_name = 'mk_gnn_ffn_d2_gnn_r8_426d24'

def setup_inputs(seed: int=0):
    np.random.seed(seed)
    _w = jnp.asarray

    def _rec_inputs():
        import jax
        import jax.numpy as jnp
        _gk = jax.random.key(seed)
        x = -0.0002117 + 1 * jax.random.normal(jax.random.fold_in(_gk, 1), (6250, 512), jnp.float32)
        src = jax.random.randint(jax.random.fold_in(_gk, 2), (100000,), 0, 6250, jnp.int32)
        dst = jnp.minimum((6250 * jax.random.uniform(jax.random.fold_in(_gk, 3), (100000,)) ** 2.0).astype(jnp.int32), 49999)
        _o = jnp.argsort(dst, stable=True)
        src = src[_o]
        dst = dst[_o]
        return (x, src, dst)
    x, src, dst = _rec_inputs()

    def _L0_gnn_setup():
        import jax, jax.numpy as jnp
        import numpy as np
        N = 6250
        E = 50000
        IN_FEATS = 512
        HEADS = 8
        OUT_FEATS = 64
        NEG_SLOPE = 0.2
        key = jax.random.key(seed)
        ks = jax.random.split(key, 12)
        HF = HEADS * OUT_FEATS
        s = 1.0 / np.sqrt(IN_FEATS)
        inp = {'feat': jax.random.normal(ks[0], (N, IN_FEATS), dtype=jnp.float32), 'src': jax.random.randint(ks[1], (E,), 0, N, dtype=jnp.int32), 'dst': jax.random.randint(ks[2], (E,), 0, N, dtype=jnp.int32), 'W_src': jax.random.normal(ks[3], (IN_FEATS, HF), dtype=jnp.float32) * s, 'b_src': jax.random.normal(ks[4], (HF,), dtype=jnp.float32) * 0.01, 'W_dst': jax.random.normal(ks[5], (IN_FEATS, HF), dtype=jnp.float32) * s, 'b_dst': jax.random.normal(ks[6], (HF,), dtype=jnp.float32) * 0.01, 'W_val': jax.random.normal(ks[7], (IN_FEATS, HF), dtype=jnp.float32) * s, 'b_val': jax.random.normal(ks[8], (HF,), dtype=jnp.float32) * 0.01, 'attn_l': jax.random.normal(ks[9], (HEADS, OUT_FEATS), dtype=jnp.float32) * 0.1, 'attn_r': jax.random.normal(ks[10], (HEADS, OUT_FEATS), dtype=jnp.float32) * 0.1}
        return inp
    _L0_gnn_all = _L0_gnn_setup()
    _L0_gnn_in = {k: v for k, v in _L0_gnn_all.items() if k in ('W_src', 'b_src', 'W_dst', 'b_dst', 'W_val', 'b_val', 'attn_l', 'attn_r')}
    del _L0_gnn_all

    def _L0_ffn_setup():
        import jax, jax.numpy as jnp
        import numpy as np

        def _haar_dwt2(x):
            a = x[:, ::2, ::2]
            b = x[:, ::2, 1::2]
            c = x[:, 1::2, ::2]
            d = x[:, 1::2, 1::2]
            ll = (a + b + c + d) * 0.5
            lh = (a + b - c - d) * 0.5
            hl = (a - b + c - d) * 0.5
            hh = (a - b - c + d) * 0.5
            return (ll, lh, hl, hh)

        def _haar_idwt2(ll, lh, hl, hh):
            a = (ll + lh + hl + hh) * 0.5
            b = (ll + lh - hl - hh) * 0.5
            c = (ll - lh + hl - hh) * 0.5
            d = (ll - lh - hl + hh) * 0.5
            B, H2, W2 = ll.shape
            out = jnp.zeros((B, 2 * H2, 2 * W2), ll.dtype)
            out = out.at[:, ::2, ::2].set(a)
            out = out.at[:, ::2, 1::2].set(b)
            out = out.at[:, 1::2, ::2].set(c)
            out = out.at[:, 1::2, 1::2].set(d)
            return out

        def _interp_linear_last(x, m):
            n = x.shape[-1]
            pos = jnp.linspace(0.0, 1.0, m, dtype=x.dtype) * (n - 1)
            i0 = jnp.clip(jnp.floor(pos).astype(jnp.int32), 0, n - 2)
            w = pos - i0.astype(x.dtype)
            return x[..., i0] * (1.0 - w) + x[..., i0 + 1] * w
        key = jax.random.key(seed)
        k0, k1, k2 = jax.random.split(key, 3)
        b, f, c, hidden = (128, 256, 512, 256)
        x = jax.random.normal(k0, (b, f, c), dtype=jnp.float32)
        fc1_w = jax.random.normal(k1, (hidden, c), dtype=jnp.float32) * 0.02
        fc1_b = jnp.zeros((hidden,), dtype=jnp.float32)
        fc2_w = jax.random.normal(k2, (c // 2, hidden), dtype=jnp.float32) * 0.02
        fc2_b = jnp.zeros((c // 2,), dtype=jnp.float32)
        return {'x': x, 'fc1_w': fc1_w, 'fc1_b': fc1_b, 'fc2_w': fc2_w, 'fc2_b': fc2_b}
    _L0_ffn_all = _L0_ffn_setup()
    _L0_ffn_in = {k: v for k, v in _L0_ffn_all.items() if k in ('fc1_w', 'fc1_b', 'fc2_w', 'fc2_b')}
    del _L0_ffn_all

    def _L1_gnn_setup():
        import jax, jax.numpy as jnp
        import numpy as np
        N, D, E = (6250, 512, 50000)
        LN_EPS = 1e-05
        key = jax.random.key(seed)
        ks = jax.random.split(key, 8)
        x = jax.random.normal(ks[0], (N, D), dtype=jnp.float32)
        edge_index = jax.random.randint(ks[1], (2, E), 0, N, dtype=jnp.int64)
        s = 1.0 / np.sqrt(D)
        W1 = jax.random.uniform(ks[2], (D, D), jnp.float32, -s, s)
        b1 = jax.random.uniform(ks[3], (D,), jnp.float32, -s, s)
        W2 = jax.random.uniform(ks[4], (D, D), jnp.float32, -s, s)
        b2 = jax.random.uniform(ks[5], (D,), jnp.float32, -s, s)
        eps = jnp.zeros((), dtype=jnp.float32)
        gamma = jnp.ones((D,), dtype=jnp.float32)
        beta = jnp.zeros((D,), dtype=jnp.float32)
        return {'x': x, 'edge_index': edge_index, 'eps': eps, 'W1': W1, 'b1': b1, 'W2': W2, 'b2': b2, 'gamma': gamma, 'beta': beta}
    _L1_gnn_all = _L1_gnn_setup()
    _L1_gnn_in = {k: v for k, v in _L1_gnn_all.items() if k in ('eps', 'W1', 'b1', 'W2', 'b2', 'gamma', 'beta')}
    del _L1_gnn_all

    def _L1_ffn_setup():
        import jax, jax.numpy as jnp
        import numpy as np
        B, T, D = (4, 1024, 512)
        E, F, CAP = (8, 256, 512)
        key = jax.random.key(seed)
        ks = jax.random.split(key, 6)
        s = 0.02
        return {'x': jax.random.normal(ks[0], (B, T, D), dtype=jnp.float32), 'Wr': jax.random.normal(ks[1], (D, E), dtype=jnp.float32) * s, 'W1': jax.random.normal(ks[2], (E, D, F), dtype=jnp.float32) * s, 'b1': jax.random.normal(ks[3], (E, F), dtype=jnp.float32) * s, 'W2': jax.random.normal(ks[4], (E, F, D), dtype=jnp.float32) * s, 'b2': jax.random.normal(ks[5], (E, D), dtype=jnp.float32) * s}
    _L1_ffn_all = _L1_ffn_setup()
    _L1_ffn_in = {k: v for k, v in _L1_ffn_all.items() if k in ('Wr', 'W1', 'b1', 'W2', 'b2')}
    del _L1_ffn_all
    return {'x': x, 'src': src, 'dst': dst, 'L0_gnn_W_src': _L0_gnn_in['W_src'], 'L0_gnn_b_src': _L0_gnn_in['b_src'], 'L0_gnn_W_dst': _L0_gnn_in['W_dst'], 'L0_gnn_b_dst': _L0_gnn_in['b_dst'], 'L0_gnn_W_val': _L0_gnn_in['W_val'], 'L0_gnn_b_val': _L0_gnn_in['b_val'], 'L0_gnn_attn_l': _L0_gnn_in['attn_l'], 'L0_gnn_attn_r': _L0_gnn_in['attn_r'], 'L0_ffn_fc1_w': _L0_ffn_in['fc1_w'], 'L0_ffn_fc1_b': _L0_ffn_in['fc1_b'], 'L0_ffn_fc2_w': _L0_ffn_in['fc2_w'], 'L0_ffn_fc2_b': _L0_ffn_in['fc2_b'], 'L1_gnn_eps': _L1_gnn_in['eps'], 'L1_gnn_W1': _L1_gnn_in['W1'], 'L1_gnn_b1': _L1_gnn_in['b1'], 'L1_gnn_W2': _L1_gnn_in['W2'], 'L1_gnn_b2': _L1_gnn_in['b2'], 'L1_gnn_gamma': _L1_gnn_in['gamma'], 'L1_gnn_beta': _L1_gnn_in['beta'], 'L1_ffn_Wr': _L1_ffn_in['Wr'], 'L1_ffn_W1': _L1_ffn_in['W1'], 'L1_ffn_b1': _L1_ffn_in['b1'], 'L1_ffn_W2': _L1_ffn_in['W2'], 'L1_ffn_b2': _L1_ffn_in['b2']}

def reference(x, src, dst, L0_gnn_W_src, L0_gnn_b_src, L0_gnn_W_dst, L0_gnn_b_dst, L0_gnn_W_val, L0_gnn_b_val, L0_gnn_attn_l, L0_gnn_attn_r, L0_ffn_fc1_w, L0_ffn_fc1_b, L0_ffn_fc2_w, L0_ffn_fc2_b, L1_gnn_eps, L1_gnn_W1, L1_gnn_b1, L1_gnn_W2, L1_gnn_b2, L1_gnn_gamma, L1_gnn_beta, L1_ffn_Wr, L1_ffn_W1, L1_ffn_b1, L1_ffn_W2, L1_ffn_b2):
    import jax
    import jax.numpy as jnp

    def _L0_gnn_ref(feat, src, dst, W_src, b_src, W_dst, b_dst, W_val, b_val, attn_l, attn_r):
        import jax, jax.numpy as jnp
        import numpy as np
        N = 6250
        E = 50000
        IN_FEATS = 512
        HEADS = 8
        OUT_FEATS = 64
        NEG_SLOPE = 0.2
        feat_src = (feat @ W_src + b_src).reshape(N, HEADS, OUT_FEATS)
        feat_dst = (feat @ W_dst + b_dst).reshape(N, HEADS, OUT_FEATS)
        feat_v = (feat @ W_val + b_val).reshape(N, HEADS, OUT_FEATS)
        el = jnp.einsum('nhf,hf->nh', feat_src, attn_l)
        er = jnp.einsum('nhf,hf->nh', feat_dst, attn_r)
        e = el[src] + er[dst]
        e = jnp.where(e >= 0, e, NEG_SLOPE * e)
        e_max = jax.ops.segment_max(e, dst, num_segments=N)
        e_max = jnp.where(jnp.isfinite(e_max), e_max, 0.0)
        exp_e = jnp.exp(e - e_max[dst])
        denom = jax.ops.segment_sum(exp_e, dst, num_segments=N)
        a = exp_e / jnp.maximum(denom[dst], 1e-16)
        msg = feat_v[src] * a[:, :, None]
        rst = jax.ops.segment_sum(msg, dst, num_segments=N)
        return rst.reshape(N, HEADS * OUT_FEATS)

    def _L0_ffn_ref(x, fc1_w, fc1_b, fc2_w, fc2_b):
        import jax, jax.numpy as jnp
        import numpy as np

        def _haar_dwt2(x):
            a = x[:, ::2, ::2]
            b = x[:, ::2, 1::2]
            c = x[:, 1::2, ::2]
            d = x[:, 1::2, 1::2]
            ll = (a + b + c + d) * 0.5
            lh = (a + b - c - d) * 0.5
            hl = (a - b + c - d) * 0.5
            hh = (a - b - c + d) * 0.5
            return (ll, lh, hl, hh)

        def _haar_idwt2(ll, lh, hl, hh):
            a = (ll + lh + hl + hh) * 0.5
            b = (ll + lh - hl - hh) * 0.5
            c = (ll - lh + hl - hh) * 0.5
            d = (ll - lh - hl + hh) * 0.5
            B, H2, W2 = ll.shape
            out = jnp.zeros((B, 2 * H2, 2 * W2), ll.dtype)
            out = out.at[:, ::2, ::2].set(a)
            out = out.at[:, ::2, 1::2].set(b)
            out = out.at[:, 1::2, ::2].set(c)
            out = out.at[:, 1::2, 1::2].set(d)
            return out

        def _interp_linear_last(x, m):
            n = x.shape[-1]
            pos = jnp.linspace(0.0, 1.0, m, dtype=x.dtype) * (n - 1)
            i0 = jnp.clip(jnp.floor(pos).astype(jnp.int32), 0, n - 2)
            w = pos - i0.astype(x.dtype)
            return x[..., i0] * (1.0 - w) + x[..., i0 + 1] * w
        b, f, c = x.shape
        ll, lh, hl, hh = _haar_dwt2(x)
        ll_up = _interp_linear_last(ll, c)
        h = jax.nn.gelu(jnp.einsum('bfc,hc->bfh', ll_up, fc1_w) + fc1_b, approximate=False)
        ll_new = jnp.einsum('bfh,oh->bfo', h, fc2_w) + fc2_b
        return _haar_idwt2(ll_new, lh, hl, hh)

    def _L1_gnn_ref(x, edge_index, eps, W1, b1, W2, b2, gamma, beta):
        import jax, jax.numpy as jnp
        import numpy as np
        N, D, E = (6250, 512, 50000)
        LN_EPS = 1e-05
        i, j = (edge_index[0], edge_index[1])
        agg = jax.ops.segment_sum(x[j], i, num_segments=x.shape[0])
        h = (1.0 + eps) * x + agg
        h = jax.nn.relu(h @ W1.T + b1)
        h = h @ W2.T + b2
        mu = jnp.mean(h, axis=-1, keepdims=True)
        var = jnp.var(h, axis=-1, keepdims=True)
        out = (h - mu) * jax.lax.rsqrt(var + LN_EPS) * gamma + beta
        return out

    def _L1_ffn_ref(x, Wr, W1, b1, W2, b2):
        import jax, jax.numpy as jnp
        import numpy as np
        B, T, D = (4, 1024, 512)
        E, F, CAP = (8, 256, 512)
        Bb, Tt, Dd = x.shape
        N = Bb * Tt
        C = min(CAP, N)
        x_flat = x.reshape(N, Dd)
        logits = x_flat @ Wr
        probs = jax.nn.softmax(logits, axis=0)
        vals, idx = jax.lax.top_k(probs.T, C)
        selected = x_flat[idx]
        h = jax.nn.gelu(jnp.einsum('ecd,edf->ecf', selected, W1) + b1[:, None, :], approximate=False)
        out_e = jnp.einsum('ecf,efd->ecd', h, W2) + b2[:, None, :]
        weighted = vals[..., None] * out_e
        output = jnp.zeros_like(x_flat).at[idx.reshape(-1)].add(weighted.reshape(-1, Dd))
        return output.reshape(Bb, Tt, Dd)
    edge_index = jnp.stack([src, dst])
    x = x + _L0_gnn_ref(_layernorm(x, axis=-1), src, dst, L0_gnn_W_src, L0_gnn_b_src, L0_gnn_W_dst, L0_gnn_b_dst, L0_gnn_W_val, L0_gnn_b_val, L0_gnn_attn_l, L0_gnn_attn_r)
    x = x + _L0_ffn_ref(_layernorm(x, axis=-1)[None], L0_ffn_fc1_w, L0_ffn_fc1_b, L0_ffn_fc2_w, L0_ffn_fc2_b)[0]
    x = x + _L1_gnn_ref(_layernorm(x, axis=-1), edge_index, L1_gnn_eps, L1_gnn_W1, L1_gnn_b1, L1_gnn_W2, L1_gnn_b2, L1_gnn_gamma, L1_gnn_beta)
    x = x + _L1_ffn_ref(_layernorm(x, axis=-1)[None], L1_ffn_Wr, L1_ffn_W1, L1_ffn_b1, L1_ffn_W2, L1_ffn_b2)[0]
    return x

_drawn_inputs = setup_inputs


def setup_inputs(seed=0):
    import zlib

    import numpy as np

    out = dict(_drawn_inputs(seed))
    spreads = {'L0_ffn_fc1_b': (0.0, 0.8),
     'L0_ffn_fc2_b': (0.0, 0.1),
     'L1_gnn_gamma': (1.0, 0.2),
     'L1_gnn_beta': (0.0, 0.1)}
    factors = {'L0_gnn_b_src': 64.0,
     'L0_gnn_b_dst': 64.0,
     'L0_gnn_b_val': 3.362,
     'L0_ffn_fc1_w': 3.137,
     'L1_gnn_b1': 8.0,
     'L1_gnn_b2': 4.29,
     'L1_ffn_Wr': 8.0,
     'L1_ffn_W1': 8.0,
     'L1_ffn_b1': 200.0,
     'L1_ffn_W2': 8.0,
     'L1_ffn_b2': 200.0}
    for name, (base, spread) in spreads.items():
        noise = np.random.default_rng([zlib.crc32(name.encode()), seed]).standard_normal(out[name].shape)
        drawn = base * np.exp(spread * noise) if base else spread * noise
        out[name] = jnp.asarray(drawn.astype(out[name].dtype))
    for name, factor in factors.items():
        out[name] = (out[name] * factor).astype(out[name].dtype)
    return out
```

```python
from contextlib import ExitStack

import numpy as np
import concourse.bass as bass
import concourse.mybir as mybir

ALU = mybir.AluOpType
ACT = mybir.ActivationFunctionType
F32 = mybir.dt.float32
I32 = mybir.dt.int32
AX = mybir.AxisListType

P = 128
N, D, H = 6250, 512, 8
F = D // H
NT = 50
NP = NT * P
T = -(-N // P)
NE = 100000
EC = 784
EP = P * EC
PAIR = 2 * P
ROWS = EP // PAIR
PAD_NODE = T * P - 1
NPAIR = 440
QN = NPAIR // 2
QI = 4
ITER = QN // QI
WL = 512
W = D + H
EPS = 1e-5
FAR = 30000
HID = 256
NX, FX, CAP = 8, 256, 512
SEG = NP // 16
assert ROWS + T - 1 <= NPAIR and ITER * QI * 2 == NPAIR


class Steps:

    def __init__(self, eng, sem, g=None):
        self.g = g
        self.eng, self.sem, self.base, self.k, self.i, self.per = eng, sem, 0, 0, None, 0

    def value(self):
        return self.base + self.k if self.i is None else self.i * self.per + (self.base + self.k)

    def mark(self, ins):
        self.k += 1
        ins.then_inc(self.sem, 1)
        return self.value()

    def link(self, ins):
        self.mark(ins)
        self.eng.wait_ge(self.sem, self.value())

    def enter(self, i, per):
        self.base, self.k, self.i, self.per = self.base + self.k, 0, i, per

    def leave(self, n):
        assert self.k == self.per, (self.k, self.per)
        self.base, self.k, self.i = self.base + self.per * n, 0, None


def fold_consts(nc, g):
    with ExitStack() as ctx:
        sb, sem, ps = g.maker(ctx)
        loaded, pool_done, dve_done, fold_ready = sem("c_loaded"), sem("c_pool"), sem("c_dve"), sem("c_fold")
        w_raw = g.acc[:, 0:2048].rearrange("p (c n) -> p c n", c=4)
        w_tmp = g.acc[:, 2048:4096].rearrange("p (c n) -> p c n", c=4)
        att = sb("att", [P, 2 * D])
        brow = sb("brow", [P, 2 * D])
        ut = g.acc[:, 4096:5120].rearrange("p (c n) -> p c n", c=4)
        f1 = g.acc[:, 5120:6144].rearrange("p (c n) -> p c n", c=4)
        ramp = sb("ramp", [P, P])
        pw = ps("pw", [P, 2, HID])
        w_dst_raw = g.acc[:, 6144:8192].rearrange("p (c n) -> p c n", c=4)
        block = ctx.enter_context(nc.Block())

        @block.sync
        def _(sp):
            sp.dma_start(w_raw, g.W_src.rearrange("(c p) n -> p c n", p=P)).then_inc(loaded, 16)
            sp.dma_start(w_dst_raw, g.W_dst.rearrange("(c p) n -> p c n", p=P)).then_inc(loaded, 16)
            for j, (a, b) in enumerate(((g.attn_l, g.b_src), (g.attn_r, g.b_dst))):
                sp.dma_start(att[:, j * D:(j + 1) * D], a.to_broadcast([P, D])).then_inc(loaded, 16)
                sp.dma_start(brow[:, j * D:(j + 1) * D], b.to_broadcast([P, D])).then_inc(loaded, 16)
            sp.dma_start(ut, g.interp.rearrange("(c p) n -> p c n", p=P)).then_inc(loaded, 16)
            sp.dma_start(f1, g.fc1T.rearrange("(c p) n -> p c n", p=P)).then_inc(loaded, 16)
            sp.dma_start(g.fc1b[:], g.fc1_b).then_inc(loaded, 16)
            sp.dma_start(g.fc2T[:], g.fc2T_d.rearrange("(c p) n -> p c n", p=P)).then_inc(loaded, 16)
            sp.dma_start(g.fc2b[:], g.fc2_b).then_inc(loaded, 16)
            sp.dma_start(g.Wv[:, :, 0:D], g.W_val.rearrange("(c p) n -> p c n", p=P)).then_inc(loaded, 16)
            sp.dma_start(g.bv[:, 0:D], g.b_val.to_broadcast([P, D])).then_inc(loaded, 16)
            sp.dma_start(g.epsb[:], g.eps.to_broadcast([P, 1])).then_inc(loaded, 16)
            sp.wait_ge(loaded, 16 * 14)

        @block.gpsimd
        def _(pool):
            st = Steps(pool, pool_done)
            st.mark(pool.memset(g.ident[:], 0.0))
            st.mark(pool.memset(g.ones[:], 1.0))
            st.mark(pool.memset(g.ln_eps[:], EPS))
            st.mark(pool.memset(g.upper[:], 1.0))
            st.mark(pool.memset(g.pairup[:], 0.5))
            st.mark(pool.memset(g.group[:], 1.0))
            st.mark(pool.iota(g.iota[:], pattern=[[1, P]], base=0, channel_multiplier=0,
                              allow_small_or_imprecise_dtypes=True))
            pool.wait_ge(pool_done, st.value())
            st.mark(pool.affine_select(out=g.ident[:], in_=g.ident[:], compare_op=ALU.not_equal, fill=1.0, base=0,
                                       pattern=[[-1, P]], channel_multiplier=1))
            st.mark(pool.affine_select(out=g.upper[:], in_=g.upper[:], compare_op=ALU.is_gt, fill=0.0, base=0,
                                       pattern=[[1, P]], channel_multiplier=-1))
            v = g.pairup[:]
            st.link(pool.affine_select(out=v, in_=v, compare_op=ALU.is_ge, fill=0.0, base=0,
                                       pattern=[[-2, P // 2]], channel_multiplier=1))
            st.mark(pool.affine_select(out=v, in_=v, compare_op=ALU.is_ge, fill=0.0, base=1,
                                       pattern=[[2, P // 2]], channel_multiplier=-1))
            v = g.group[:].rearrange("p (a b) -> p a b", b=16)
            st.link(pool.affine_select(out=v, in_=v, compare_op=ALU.is_ge, fill=0.0, base=0,
                                       pattern=[[-16, 8], [0, 16]], channel_multiplier=1))
            st.link(pool.affine_select(out=v, in_=v, compare_op=ALU.is_ge, fill=0.0, base=15,
                                       pattern=[[16, 8], [0, 16]], channel_multiplier=-1))
            st.link(pool.memset(g.expand[:], 1.0))
            v = g.expand[:]
            st.link(pool.affine_select(out=v, in_=v, compare_op=ALU.is_ge, fill=0.0, base=0,
                                       pattern=[[1, P]], channel_multiplier=-16))
            st.link(pool.affine_select(out=v, in_=v, compare_op=ALU.is_ge, fill=0.0, base=15,
                                       pattern=[[-1, P]], channel_multiplier=16))

        @block.vector
        def _(dve):
            st = Steps(dve, dve_done)
            dve.wait_ge(loaded, 16 * 14)
            for j, w in enumerate((w_raw, w_dst_raw)):
                a = att[:, j * D:(j + 1) * D].unsqueeze(1).to_broadcast([P, 4, D])
                st.link(dve.tensor_tensor(w_tmp, w, a, ALU.mult))
                st.link(dve.tensor_reduce(g.Wlr[:, :, j * H:(j + 1) * H],
                                          w_tmp.rearrange("p c (h f) -> p c h f", h=H), AX.X, ALU.add))
                b = brow[:, j * D:(j + 1) * D]
                st.link(dve.tensor_tensor(b, b, att[:, j * D:(j + 1) * D], ALU.mult))
                st.link(dve.tensor_reduce(g.blr[:, j * H:(j + 1) * H],
                                          b.rearrange("p (h f) -> p h f", h=H), AX.X, ALU.add))
            dve.wait_ge(pool_done, 16)
            v = g.unpair[:].rearrange("p (a b) -> p a b", b=2)
            st.link(dve.tensor_scalar(v, g.pairup[:].unsqueeze(2).to_broadcast([P, P // 2, 2]), -1.0, None, ALU.mult))
            st.link(dve.tensor_tensor(g.below[:], g.upper[:], g.group[:], ALU.mult))
            st.link(dve.tensor_scalar(g.epsb[:], g.epsb[:], 1.0, None, ALU.add))
            dve.wait_ge(fold_ready, 1)
            st.link(dve.tensor_copy(g.Wf[:], pw[:]))

        @block.tensor
        def _(pe):
            pe.wait_ge(loaded, 16 * 14)
            for jb in range(2):
                for c in range(4):
                    last = pe.matmul(pw[:, jb, :], ut[:, c, jb * P:(jb + 1) * P], f1[:, c, :],
                                     start=(c == 0), stop=(c == 3))
            last.then_inc(fold_ready, 1)


def plan_edges(nc, g):
    with ExitStack() as ctx:
        sb, sem, ps = g.maker(ctx)
        loaded, step, filled, prefilled = sem("p_loaded"), sem("p_step"), sem("p_filled"), sem("p_prefilled")
        recs, counted, summed = sem("p_recs"), sem("p_counted"), sem("p_summed")
        tiles_out, planned, tiles_in = sem("p_tiles_out"), sem("p_planned"), sem("p_tiles_in")
        pool_io, rows_in = sem("p_pool_io"), g.sw["rows"][0]
        A = g.acc
        src_i, dst_i = A[:, 0:EC].bitcast(I32), A[:, EC:2 * EC].bitcast(I32)
        hs, hd = A[:, 4 * EC:5 * EC], A[:, 5 * EC:6 * EC]
        mask, run, pos = A[:, 6 * EC:7 * EC], A[:, 7 * EC:8 * EC], A[:, 8 * EC:9 * EC]
        zeros, tmp = A[:, 10 * EC:11 * EC], A[:, 11 * EC:12 * EC]
        fill = A[:, 12 * EC:12 * EC + 2048].bitcast(I32)
        cnt = sb("cnt", [P, 2 * T])
        tot = sb("tot", [P, 2 * T])
        base = sb("base", [P, T])
        s = [sb(f"pl{i}", [P, T]) for i in range(8)]
        si = sb("pli", [P, T], I32)
        kcol = sb("kcol", [P, 4])
        tk = sb("tk", [P, 2, 4])
        tki = sb("tki", [P, 2, 4], I32)
        rowf = sb("rowf", [P, 4])
        rowi = sb("rowi", [P, 4], I32)
        junk = sb("junk", [P, T])
        tiota = sb("tiota", [P, T])
        pt = ps("pt", [P, 2 * T])
        pb = ps("pb", [P, T])
        block = ctx.enter_context(nc.Block())

        @block.sync
        def _(sp):
            sp.dma_start(src_i, g.src.rearrange("(p c) -> p c", p=P)).then_inc(loaded, 16)
            sp.dma_start(dst_i, g.dst.rearrange("(p c) -> p c", p=P)).then_inc(loaded, 16)
            sp.wait_ge(filled, 1)
            sp.dma_start(g.by_src.rearrange("(p k) c -> p (k c)", p=P), fill).then_inc(prefilled, 16)
            sp.wait_ge(planned, 1)
            for layer in range(2):
                sp.dma_start(g.tiles_d[layer, :].rearrange("(p b) -> p b", p=P), tki[:, layer, :])\
                  .then_inc(tiles_out, 16)
            sp.wait_ge(tiles_out, 32)
            sp.dma_start(g.tiles[:], g.tiles_d.rearrange("a k -> (a k)").unsqueeze(0)).then_inc(tiles_in, 16)
            sp.wait_ge(tiles_in, 16)
            sp.wait_ge(prefilled, 16)

        @block.gpsimd
        def _(pool):
            st = Steps(pool, pool_io)
            st.mark(pool.iota(tiota[:], pattern=[[1, T]], base=0, channel_multiplier=0,
                              allow_small_or_imprecise_dtypes=True))
            st.mark(pool.iota(kcol[:], pattern=[[1, 4]], base=0, channel_multiplier=4,
                              allow_small_or_imprecise_dtypes=True))
            f = fill.rearrange("p (k c) -> p k c", c=2)
            pool.memset(f[:, :, 1], 0)
            pool.memset(f[:, :, 0], FAR).then_inc(filled, 1)
            st.mark(pool.memset(zeros, 0.0))
            pool.wait_ge(loaded, 32)
            r = g.rec
            pool.tensor_copy(r[:, :, 0], src_i)
            st.mark(pool.tensor_copy(r[:, :, 1], dst_i))
            pool.wait_ge(planned, 1)
            for arr, out in ((g.src, g.rows[:, :, 0]), (g.dst, g.rows[:, :, 1])):
                for b in range(4):
                    pool.indirect_dma_start(out[:, b, :], None, arr.rearrange("(r e) -> r e", e=PAIR),
                                            bass.IndirectOffsetOnAxis(ap=rowi[:, b:b + 1], axis=0))\
                        .then_inc(rows_in, 16)
            pool.wait_ge(rows_in, 16 * 8)

        @block.tensor
        def _(pe):
            pe.wait_ge(counted, 1)
            pe.matmul(pt[:], g.ones[:], cnt[:], start=True, stop=True)
            pe.matmul(pb[:], g.upper[:], cnt[:, 0:T], start=True, stop=True).then_inc(summed, 1)

        @block.vector
        def _(dve):
            st = Steps(dve, step, g)
            dve.wait_ge(loaded, 32)
            dve.wait_ge(pool_io, 4)
            hi_s, hi_d = mask.bitcast(I32), run.bitcast(I32)
            st.mark(dve.tensor_scalar(hi_s, src_i, 7, None, ALU.logical_shift_right))
            st.link(dve.tensor_scalar(hi_d, dst_i, 7, None, ALU.logical_shift_right))
            st.mark(dve.tensor_copy(hs, hi_s))
            st.mark(dve.tensor_copy(hd, hi_d))
            st.link(dve.memset(pos, 0.0))
            with dve.Fori(0, T) as b:
                st.enter(b, 2)
                for h, o in ((hs, 0), (hd, T)):
                    out = tmp if o else run
                    st.link(dve.tensor_scalar(out, h, tiota[:, bass.ds(b, 1)], 0.0, ALU.is_equal, ALU.add,
                                              accum_out=cnt[:, bass.ds(b + o, 1)]))
            st.leave(T)
            dve.sem_inc(counted, 1)
            dve.wait_ge(summed, 1)
            st.mark(dve.tensor_copy(tot[:], pt[:]))
            st.link(dve.tensor_copy(base[:], pb[:]))
            z = zeros[:, 0:T]

            def shift(out, x, add):
                st.link(dve.tensor_scalar(out, x, float(add), None, ALU.add))
                st.link(dve.tensor_copy(si[:], out))
                st.link(dve.tensor_scalar(si[:], si[:], 8, None, ALU.logical_shift_right))
                st.link(dve.tensor_copy(out, si[:]))

            n1, end1, n0, end0, first, a, d0, dd = (x[:] for x in s)
            shift(n1, tot[:, 0:T], PAIR - 1)
            st.link(dve.tensor_tensor_scan(end1, n1, z, 0.0, ALU.add, ALU.add))
            st.link(dve.tensor_tensor(a, end1, n1, ALU.subtract))
            st.link(dve.tensor_scalar(a, a, float(PAIR), -1.0, ALU.mult, ALU.add))
            st.link(dve.tensor_tensor(base[:], base[:], a, ALU.add))
            te = tot[:, T:2 * T]
            st.link(dve.tensor_tensor_scan(end0, te, z, 0.0, ALU.add, ALU.add))
            st.link(dve.tensor_tensor(a, end0, te, ALU.subtract))
            st.link(dve.tensor_scalar(n0, a, 1.0, None, ALU.add))
            shift(first, a, 0)
            st.link(dve.tensor_tensor(a, end0, n0, ALU.max))
            shift(n0, a, -1)
            st.link(dve.tensor_tensor(n0, n0, first, ALU.subtract))
            st.link(dve.tensor_scalar(n0, n0, 1.0, None, ALU.add))
            st.link(dve.tensor_tensor_scan(end0, n0, z, 0.0, ALU.add, ALU.add))
            st.link(dve.tensor_tensor(d0, end0, n0, ALU.subtract))
            st.link(dve.tensor_tensor(d0, first, d0, ALU.subtract))
            st.link(dve.memset(dd, 0.0))
            st.link(dve.tensor_tensor(dd[:, 0:T - 1], d0[:, 1:T], d0[:, 0:T - 1], ALU.subtract))
            for b in range(4):
                k = kcol[:, b:b + 1]
                for layer, end in ((0, end0), (1, end1)):
                    st.link(dve.tensor_scalar(junk[:], end, k, 0.0, ALU.is_le, ALU.add,
                                              accum_out=tk[:, layer, b:b + 1]))
                    if layer == 0:
                        st.link(dve.tensor_tensor_reduce(out=junk[:], in0=junk[:], in1=dd, scale=1.0, scalar=0.0,
                                                         op0=ALU.mult, op1=ALU.add, accum_out=rowf[:, b:b + 1]))
            st.link(dve.tensor_tensor(rowf[:], rowf[:], kcol[:], ALU.add))
            st.link(dve.tensor_scalar(rowf[:], rowf[:], d0[:, 0:1], float(ROWS - 1), ALU.add, ALU.min))
            st.link(dve.tensor_copy(rowi[:], rowf[:]))
            st.link(dve.tensor_scalar(g.tile_base[:], tk[:], float(P), None, ALU.mult))
            st.link(dve.tensor_scalar(tk[:], tk[:], float(T - 1), None, ALU.min))
            st.link(dve.tensor_copy(tki[:], tk[:]))
            dve.sem_inc(planned, 1)
            with dve.Fori(0, T) as b:
                st.enter(b, 4)
                key = tiota[:, bass.ds(b, 1)]
                st.link(dve.tensor_scalar(mask, hs, key, None, ALU.is_equal))
                st.link(dve.tensor_tensor_scan(run, mask, zeros, base[:, bass.ds(b, 1)], ALU.add, ALU.add))
                st.link(dve.tensor_tensor(tmp, mask, run, ALU.mult))
                st.link(dve.tensor_tensor(pos, pos, tmp, ALU.add))
            st.leave(T)
            st.link(dve.tensor_copy(g.place[:], pos))


def build_index(nc, g, layer):
    with ExitStack() as ctx:
        sb, sem, ps = g.maker(ctx)
        loaded, conv, turned, moved = (sem(f"x{layer}_{n}") for n in ("loaded", "conv", "turned", "moved"))
        vals = g.acc[:, 16000:18048].rearrange("p (b w e) -> p b w e", b=4, w=2)
        raw = g.rows[:] if layer == 0 else g.rows[:].rearrange("p b w e -> p b (w e)").rearrange(
            "p b (e w) -> p b w e", w=2)
        pt = [ps(f"pi{layer}{u}", [P, 4, P]) for u in range(4)]
        block = ctx.enter_context(nc.Block())
        if layer == 1:
            @block.sync
            def _(sp):
                sp.dma_start(g.rows[:].rearrange("p b w e -> p (b w e)"),
                             g.by_src.rearrange("(p e) w -> p (e w)", p=P)).then_inc(loaded, 16)

        @block.vector
        def _(dve):
            if layer == 1:
                dve.wait_ge(loaded, 16)
            gat, tgt = (0, 1) if layer == 0 else (1, 0)
            dve.tensor_copy(vals[:, :, 0, :], raw[:, :, gat, :]).then_inc(conv, 1)
            dve.tensor_copy(vals[:, :, 1, :], raw[:, :, tgt, :]).then_inc(conv, 1)
            dve.wait_ge(conv, 2)
            for b in range(4):
                dve.tensor_scalar(vals[:, b, 1, :], vals[:, b, 1, :], g.tile_base[:, layer, b:b + 1], None,
                                  ALU.subtract).then_inc(conv, 1)
            for b in range(4):
                dve.wait_ge(turned, b + 1)
                for w, out in ((0, g.idx), (1, g.key)):
                    dve.tensor_copy(out[:].rearrange("p (k b h) -> p b h k", b=4, h=2)[:, b, :, :],
                                    pt[b][:, 2 * w:2 * w + 2, :]).then_inc(moved, 1)
            dve.wait_ge(moved, 8)

        @block.tensor
        def _(pe):
            pe.wait_ge(conv, 6)
            for b in range(4):
                for w in range(2):
                    for h in range(2):
                        last = pe.transpose(pt[b][:, 2 * w + h, :], vals[:, b, w, h * P:(h + 1) * P], g.ident[:])
                last.then_inc(turned, 1)


def wait_apart(eng, g, sem, value):
    eng.wait_ge(sem, value)
    eng.sem_inc(g.passed, 1)


def layer_norm(dve, st, out, x, stats, mv, norm, n):
    st.mark(dve.bn_stats(stats, x))
    wait_apart(dve, st.g, st.sem, st.value())
    dve.bn_aggr(mv, stats).then_inc(norm[0], 1)
    dve.wait_ge(norm[1], n)
    st.link(dve.reciprocal(mv[:, 1:2], mv[:, 1:2]))
    return dve.tensor_scalar(out, x, mv[:, 0:1], mv[:, 1:2], ALU.subtract, ALU.mult)


def var_root(act, g, mv, norm, n):
    act.wait_ge(norm[0], n)
    act.activation(mv[:, 1:2], mv[:, 1:2], ACT.Sqrt, bias=g.ln_eps[:, 0:1]).then_inc(norm[1], 1)


def project(nc, g):
    with ExitStack() as ctx:
        sb, sem, ps = g.maker(ctx)
        x_in = [sem(f"a_x{u}") for u in range(2)]
        stored = [sem(f"a_st{u}") for u in range(2)]
        x_free, xn_ready, xT_turned, xT_copied = (sem(f"a_{n}") for n in (
            "x_free", "xn_ready", "turned", "copied"))
        v_ready, v_free, row_ready, step = (sem(f"a_{n}") for n in ("v_ready", "v_free", "row_ready", "step"))
        norm_sems = [sem("a_var"), sem("a_root")]
        emt, emb, e8 = (sem(f"a_{n}") for n in ("emt", "emb", "e8"))
        staged, scattered = sem("a_staged"), g.sw["scattered"]
        xs = [sb(f"xs{u}", [P, D]) for u in range(2)]
        xn = [sb(f"xn{u}", [P, D]) for u in range(2)]
        xT = [sb(f"xT{u}", [P, 4, P]) for u in range(2)]
        row = [sb(f"row{u}", [P, W]) for u in range(2)]
        stats, mv = sb("stats", [P, 6]), [sb(f"mv{u}", [P, 2]) for u in range(2)]
        emax = sb("emax", [P, H])
        em8, dg8 = sb("em8", [H, 1]), sb("dg8", [H, H])
        emB = sb("emB", [P, H])
        place_st = [sb(f"pls{u}", [P, 8], I32) for u in range(2)]
        rec_st = [sb(f"rcs{u}", [P, 8, 2], I32) for u in range(2)]
        pT = [ps(f"pT{u}", [P, 4, P]) for u in range(2)]
        pV = [ps(f"pV{u}", [P, D]) for u in range(2)]
        pE = [ps(f"pE{u}", [P, 2 * H]) for u in range(2)]
        pM = ps("pM", [P, P])
        block = ctx.enter_context(nc.Block())

        @block.sync
        def _(sp):
            with sp.Fori(0, NT // 2) as i:
                for u in range(2):
                    sp.wait_ge(x_free, 2 * i + (u + 1))
                    sp.dma_start(xs[u][:], g.x[bass.ds((i * 2 + u) * P, P), :]).then_inc(x_in[u], 16)

        @block.gpsimd
        def _(pool):
            with pool.Fori(0, EC // 16) as i:
                for u in range(2):
                    pool.wait_ge(scattered[u], 128 * i)
                    pool.tensor_copy(place_st[u][:], g.place[:, bass.ds(i * 16 + u * 8, 8)]).then_inc(staged, 1)
                    pool.tensor_copy(rec_st[u][:], g.rec[:, bass.ds(i * 16 + u * 8, 8), :]).then_inc(staged, 1)
                    wait_apart(pool, g, staged, 4 * i + (2 * u + 2))
                    for c in range(8):
                        pool.indirect_dma_start(g.by_src, bass.IndirectOffsetOnAxis(ap=place_st[u][:, c:c + 1], axis=0),
                                                rec_st[u][:, c, :], None).then_inc(scattered[u], 16)
            for u in range(2):
                pool.wait_ge(scattered[u], 128 * (EC // 16))

        @block.vector
        def _(dve):
            st = Steps(dve, step, g)
            dve.sem_inc(x_free, 2)
            dve.sem_inc(v_free, 2)
            st.link(dve.memset(emax[:], -3e38))

            def norm(i, u):
                dve.wait_ge(x_in[u], 16 * i + 16)
                st.link(layer_norm(dve, st, xn[u][:], xs[u][:], stats[:], mv[u][:], norm_sems, 2 * i + (u + 1)))
                dve.sem_inc(x_free, 1)
                dve.sem_inc(xn_ready, 1)

            def finish(i, u):
                n = 2 * i + u
                dve.wait_ge(v_ready, n + 1)
                dve.wait_ge(stored[u], 16 * i)
                st.mark(dve.tensor_tensor(row[u][:, 0:D], pV[u][:], g.bv[:], ALU.add))
                st.mark(dve.tensor_tensor(row[u][:, D:W], pE[u][:, 0:H], g.blr[:, 0:H], ALU.add))
                st.link(dve.tensor_tensor(g.erm[:, bass.ds((2 * i + u) * 2 * H, H)], pE[u][:, H:2 * H],
                                          g.blr[:, H:2 * H], ALU.add))
                dve.sem_inc(v_free, 1)
                dve.sem_inc(row_ready, 1)
                st.link(dve.tensor_tensor(emax[:], emax[:], row[u][:, D:W], ALU.max))

            def two(i, last):
                norm(i, 1)
                finish(i, 0)
                if not last:
                    norm(i + 1, 0)
                finish(i, 1)

            norm(0, 0)
            with dve.Fori(0, NT // 2 - 1) as i:
                st.enter(i, 14)
                two(i, False)
            st.leave(NT // 2 - 1)
            two(NT // 2 - 1, True)
            dve.sem_inc(emt, 1)
            dve.wait_ge(emt, 2)
            st.link(dve.tensor_reduce(em8[:], pM[0:H, :], AX.X, ALU.max))
            dve.tensor_scalar(dg8[:], g.ident[0:H, 0:H], em8[:, 0:1], None, ALU.mult).then_inc(e8, 1)
            dve.wait_ge(emb, 1)
            st.link(dve.tensor_copy(emB[:], pM[:, 0:H]))
            er = g.erm[:].rearrange("p (t c) -> p t c", c=2 * H)
            m, e = er[:, :, H:2 * H], er[:, :, 0:H]
            st.link(dve.tensor_tensor(m, e, emB[:].unsqueeze(1).to_broadcast([P, NT, H]), ALU.add))
            st.link(dve.scalar_tensor_tensor(out=m, in0=m, scalar=0.2, in1=m, op0=ALU.mult, op1=ALU.max))

        @block.tensor
        def _(pe):
            def turn(i, u):
                pe.wait_ge(xn_ready, 2 * i + (u + 1))
                for c in range(4):
                    last = pe.transpose(pT[u][:, c, :], xn[u][:, c * P:(c + 1) * P], g.ident[:])
                last.then_inc(xT_turned, 1)

            def mult(i, u):
                pe.wait_ge(xT_copied, 2 * i + (u + 1))
                pe.wait_ge(v_free, 2 * i + (u + 1))
                for c in range(4):
                    pe.matmul(pV[u][:], xT[u][:, c, :], g.Wv[:, c, :], start=(c == 0), stop=(c == 3))
                    last = pe.matmul(pE[u][:], xT[u][:, c, :], g.Wlr[:, c, :], start=(c == 0), stop=(c == 3))
                last.then_inc(v_ready, 1)

            def two(i, last):
                turn(i, 1)
                mult(i, 0)
                if not last:
                    turn(i + 1, 0)
                mult(i, 1)

            turn(0, 0)
            with pe.Fori(0, NT // 2 - 1) as i:
                two(i, False)
            two(NT // 2 - 1, True)
            pe.wait_ge(emt, 1)
            pe.transpose(pM[0:H, :], emax[:], g.ident[:]).then_inc(emt, 1)
            pe.wait_ge(e8, 1)
            pe.matmul(pM[:, 0:H], g.ones[0:H, :], dg8[:], start=True, stop=True).then_inc(emb, 1)

        @block.scalar
        def _(act):
            def copy(i, u):
                var_root(act, g, mv[u], norm_sems, 2 * i + (u + 1))
                act.wait_ge(xT_turned, 2 * i + (u + 1))
                if u:
                    act.wait_ge(v_ready, 2 * i)
                act.activation(xT[u][:], pT[u][:], ACT.Copy).then_inc(xT_copied, 1)

            def store(i, u):
                act.wait_ge(row_ready, 2 * i + (u + 1))
                act.dma_start(g.ve[bass.ds((i * 2 + u) * P, P), :], row[u][:]).then_inc(stored[u], 16)

            def two(i, last):
                copy(i, 1)
                store(i, 0)
                if not last:
                    copy(i + 1, 0)
                store(i, 1)

            copy(0, 0)
            with act.Fori(0, NT // 2 - 1) as i:
                two(i, False)
            two(NT // 2 - 1, True)
            for u in range(2):
                act.wait_ge(stored[u], 16 * (NT // 2))


def edge_pass(nc, g, layer):
    attend = layer == 0
    width = W if attend else D
    table = g.ve if attend else g.z
    AHEAD = 3 if attend else 2
    ADDS = 2 if attend else 1
    CH = 4 * QI
    with ExitStack() as ctx:
        sb, sem, ps = g.maker(ctx)
        n_ = f"e{layer}_"
        got = g.sw[f"got{layer}"]
        staged, zeroed = sem(n_ + "staged"), sem(n_ + "zeroed")
        hot, hot_turned, hot_copied, scored, logit, weight, scaled = (sem(n_ + x) for x in (
            "hot", "turned", "copied", "scored", "logit", "weight", "scaled"))
        summed, chain, acc_step, hot_free = (sem(n_ + x) for x in (
            "summed", "chain", "acc", "hfree"))
        G = sb(f"G{layer}", [P, CH, width])
        idx_st = sb(f"idx_st{layer}", [P, CH], I32)
        S = [sb(f"S{layer}{u}", [P, 4, P]) for u in range(QI)]
        NA = 2 if attend else 4
        pA = [ps(f"pA{layer}{u}", [P, D]) for u in range(NA)]
        if attend:
            ST = [sb(f"ST{u}", [P, 4, P]) for u in range(2)]
            sc = [sb(f"sc{u}", [P, 4, H]) for u in range(2)]
            pS = [ps(f"pS{u}", [P, 4, P]) for u in range(2)]
            pE = [ps(f"pEd{u}", [P, 4, 2 * H]) for u in range(2)]
            pD = [ps(f"pD{u}", [P, H]) for u in range(NA)]
        block = ctx.enter_context(nc.Block())

        def tiles_of(engine, i, q):
            ids = g.tiles[0:1, bass.ds(i * (2 * QI) + (layer * WL + 2 * q), 2)]
            return nc.values_load_multi_w_load_instructions(ids, engines=[engine], min_val=0, max_val=T - 1)[1]

        def laps(eng, body):
            body(0, True, False)
            with eng.Fori(1, ITER - 1) as i:
                body(i, False, False)
            body(ITER - 1, False, True)

        @block.gpsimd
        def _(pool):
            def lap(i, first, last):
                for h in range(2):
                    sl = slice(h * 8, h * 8 + 8)
                    if not first:
                        for u in range(h * 8, h * 8 + 8):
                            pool.wait_ge(got[u], 16 * i)
                    pool.tensor_copy(idx_st[:, sl], g.idx[:, bass.ds(i * CH + h * 8, 8)]).then_inc(staged, 1)
                    wait_apart(pool, g, staged, 2 * i + (h + 1))
                    for u in range(h * 8, h * 8 + 8):
                        if not first and u % 4 == 0:
                            wait_apart(pool, g, summed, (i - 1) * (2 * QI) + (u // 2 + 2))
                        pool.indirect_dma_start(G[:, u, :], None, table,
                                                bass.IndirectOffsetOnAxis(ap=idx_st[:, u:u + 1], axis=0))\
                            .then_inc(got[u], 16)

            laps(pool, lap)

        @block.vector
        def _(dve):
            dve.memset(g.acc[:], 0.0).then_inc(zeroed, 1)
            dve.wait_ge(zeroed, 1)

            def one_hot(i, q):
                if not (isinstance(i, int) and i == 0):
                    dve.wait_ge(summed, (i - 1) * (2 * QI) + (2 * q + 2))
                k = g.key[:, bass.ds(i * CH + 4 * q, 4)].unsqueeze(2).to_broadcast([P, 4, P])
                dve.tensor_tensor(S[q][:], g.iota[:].unsqueeze(1).to_broadcast([P, 4, P]), k, ALU.is_equal)\
                   .then_inc(hot, 1)

            def score(i, q, part):
                Q = i * QI + q
                t, e = sc[q % 2][:], pE[q % 2][:]
                if part == 0:
                    for u in range(4 * q, 4 * q + 4):
                        dve.wait_ge(got[u], 16 * i + 16)
                    dve.wait_ge(scored, Q + 1)
                    dve.tensor_tensor(t, G[:, 4 * q:4 * q + 4, D:W], e[:, :, 0:H], ALU.add).then_inc(chain, 1)
                elif part == 1:
                    dve.wait_ge(chain, 2 * Q + 1)
                    dve.scalar_tensor_tensor(out=t, in0=t, scalar=0.2, in1=t, op0=ALU.mult, op1=ALU.max)\
                       .then_inc(chain, 1)
                else:
                    dve.wait_ge(chain, 2 * Q + 2)
                    dve.tensor_tensor(t, t, e[:, :, H:2 * H], ALU.subtract).then_inc(logit, 1)

            def scale(i, q, u):
                dve.wait_ge(weight, i * QI + (q + 1))
                v = G[:, 4 * q + u, 0:D].rearrange("p (h f) -> p h f", h=H)
                dve.tensor_tensor(v, v, G[:, 4 * q + u, D:W].unsqueeze(2).to_broadcast([P, H, F]), ALU.mult)\
                   .then_inc(scaled, 1)

            def add(i, q, p, t):
                k = i * (2 * QI) + (2 * q + p)
                b = (2 * q + p) % NA
                dve.wait_ge(summed, k + 1)
                if not (isinstance(k, int) and k == 0):
                    dve.wait_ge(acc_step, k * ADDS)
                a = g.acc[:, bass.ds(t * W, D)]
                dve.tensor_tensor(a, a, pA[b][:], ALU.add).then_inc(acc_step, 1)
                if attend:
                    a = g.acc[:, bass.ds(t * W + D, H)]
                    dve.tensor_tensor(a, a, pD[b][:], ALU.add).then_inc(acc_step, 1)

            def lap(i, first, last):
                for q in range(QI):
                    prev = (i, q - 1) if q else (i - 1, QI - 1)
                    adds = not (first and q == 0)
                    if adds:
                        tiles = tiles_of(mybir.EngineType.DVE, *prev)
                        add(*prev, 0, tiles[0])
                    if not (last and q >= QI - AHEAD):
                        one_hot(i + (q + AHEAD) // QI, (q + AHEAD) % QI)
                    if adds:
                        add(*prev, 1, tiles[1])
                    if attend:
                        weighs, scores = not (last and q >= QI - 1), not (last and q >= QI - 2)
                        for u in range(4):
                            if scores and u < 3:
                                score(i + (q + 2) // QI, (q + 2) % QI, u)
                            if weighs:
                                scale(i + (q + 1) // QI, (q + 1) % QI, u)

            for q in range(AHEAD):
                one_hot(0, q)
            if attend:
                for q in range(2):
                    for part in range(3):
                        score(0, q, part)
                for u in range(4):
                    scale(0, 0, u)
            laps(dve, lap)
            tiles = tiles_of(mybir.EngineType.DVE, ITER - 1, QI - 1)
            for p in range(2):
                add(ITER - 1, QI - 1, p, tiles[p])

        @block.tensor
        def _(pe):
            def turn(i, q):
                Q = i * QI + q
                pe.wait_ge(hot, Q + 1)
                for u in range(4):
                    last = pe.transpose(pS[q % 2][:, u, :], S[q][:, u, :], g.ident[:])
                last.then_inc(hot_turned, 1)

            def spread(i, q):
                tiles = tiles_of(mybir.EngineType.PE, i, q)
                pe.wait_ge(hot_copied, i * QI + (q + 1))
                for p in range(2):
                    t = tiles[p]
                    for u in (2 * p, 2 * p + 1):
                        last = pe.matmul(pE[q % 2][:, u, :], ST[q % 2][:, u, :], g.erm[:, bass.ds(t * 2 * H, 2 * H)],
                                         start=True, stop=True)
                last.then_inc(scored, 1)

            def reduce(i, q, p):
                k = 2 * q + p
                if not (isinstance(i, int) and i == 0 and k < NA):
                    pe.wait_ge(acc_step, (i * (2 * QI) + (k - NA + 1)) * ADDS)
                if attend:
                    pe.wait_ge(scaled, i * CH + (2 * k + 2))
                else:
                    pe.wait_ge(hot, i * QI + (q + 1))
                    for u in (0, 1):
                        pe.wait_ge(got[2 * k + u], 16 * i + 16)
                for u in (0, 1):
                    s = S[q][:, 2 * p + u, :]
                    last = pe.matmul(pA[k % NA][:], s, G[:, 2 * k + u, 0:D], start=(u == 0), stop=(u == 1))
                    if attend:
                        last = pe.matmul(pD[k % NA][:], s, G[:, 2 * k + u, D:W], start=(u == 0), stop=(u == 1))
                last.then_inc(summed, 1)

            def lap(i, first, last):
                for q in range(QI):
                    if attend and not (last and q >= QI - 2):
                        spread(i + (q + 2) // QI, (q + 2) % QI)
                    reduce(i, q, 0)
                    if attend and not (last and q >= QI - 3):
                        turn(i + (q + 3) // QI, (q + 3) % QI)
                    reduce(i, q, 1)

            if attend:
                turn(0, 0)
                turn(0, 1)
                spread(0, 0)
                turn(0, 2)
                spread(0, 1)
            laps(pe, lap)

        if attend:
            @block.scalar
            def _(act):
                def copy(i, q):
                    act.wait_ge(hot_turned, i * QI + (q + 1))
                    if not (isinstance(i, int) and i == 0 and q < 2):
                        act.wait_ge(scored, i * QI + (q - 1))
                    act.activation(ST[q % 2][:], pS[q % 2][:], ACT.Copy).then_inc(hot_copied, 1)

                def weigh(i, q):
                    act.wait_ge(logit, i * QI + (q + 1))
                    act.activation(G[:, 4 * q:4 * q + 4, D:W], sc[q % 2][:], ACT.Exp).then_inc(weight, 1)

                def lap(i, first, last):
                    for q in range(QI):
                        if not (last and q >= QI - 3):
                            copy(i + (q + 3) // QI, (q + 3) % QI)
                        if not (last and q >= QI - 2):
                            weigh(i + (q + 2) // QI, (q + 2) % QI)

                copy(0, 0)
                copy(0, 1)
                weigh(0, 0)
                copy(0, 2)
                weigh(0, 1)
                laps(act, lap)


def wavelet_ffn(nc, g):
    with ExitStack() as ctx:
        sb, sem, ps = g.maker(ctx)
        x_in, stored = ([sem(f"b_{n}{u}") for u in range(2)] for n in ("x", "st"))
        x_free, step, yc_ready, sum_ready, s_free = (sem(f"b_{n}") for n in (
            "x_free", "step", "yc_ready", "sum_ready", "s_free"))
        low, low_copied, hid, hid_done, delta_ready, row_ready = (sem(f"b_{n}") for n in (
            "low", "low_copied", "hid", "hid_done", "delta", "row_ready"))
        norm1, norm2 = [sem("b_var1"), sem("b_inv1")], [sem("b_var2"), sem("b_inv2")]
        xs, x1, y, s, x2, z = ([sb(f"w{n}{u}", [P, D]) for u in range(2)] for n in ("xs", "x1", "y", "s", "x2", "z"))
        yc = [sb(f"yc{u}", [P, HID]) for u in range(2)]
        lT = [sb(f"lT{u}", [P, 2, P // 2]) for u in range(2)]
        hT = [sb(f"hT{u}", [P, 2, P]) for u in range(2)]
        rd, stats, mv1, mv2 = sb("rd", [P, H]), sb("wstats", [P, 6]), sb("wmv1", [P, 2]), sb("wmv2", [P, 2])
        pL = [ps(f"pL{u}", [P, 2, P // 2]) for u in range(2)]
        pH = [ps(f"pH{u}", [P, 2, P // 2]) for u in range(2)]
        pX = [ps(f"pX{u}", [P, HID]) for u in range(2)]
        block = ctx.enter_context(nc.Block())

        @block.sync
        def _(sp):
            with sp.Fori(0, NT // 2) as i:
                for u in range(2):
                    sp.wait_ge(x_free, 2 * i + (u + 1))
                    sp.dma_start(xs[u][:], g.x[bass.ds((i * 2 + u) * P, P), :]).then_inc(x_in[u], 16)

        @block.vector
        def _(dve):
            st = Steps(dve, step, g)
            dve.sem_inc(x_free, 2)

            def front(i, u):
                n = 2 * i + u
                den = g.acc[:, bass.ds((2 * i + u) * W + D, H)]
                st.link(dve.tensor_scalar(rd[:], den, 1e-30, None, ALU.max))
                st.link(dve.reciprocal(rd[:], rd[:]))
                a = g.acc[:, bass.ds((2 * i + u) * W, D)].rearrange("p (h f) -> p h f", h=H)
                st.link(dve.tensor_tensor(x1[u][:].rearrange("p (h f) -> p h f", h=H), a,
                                          rd[:].unsqueeze(2).to_broadcast([P, H, F]), ALU.mult))
                dve.wait_ge(x_in[u], 16 * i + 16)
                st.link(dve.tensor_tensor(x1[u][:], x1[u][:], xs[u][:], ALU.add))
                dve.sem_inc(x_free, 1)
                st.link(layer_norm(dve, st, y[u][:], x1[u][:], stats[:], mv1[:], norm1, n + 1))
                v = y[u][:].rearrange("p (j c) -> p j c", c=2)
                st.link(dve.tensor_tensor(yc[u][:], v[:, :, 0], v[:, :, 1], ALU.add))
                dve.sem_inc(yc_ready, 1)

            def back(i, u):
                n = 2 * i + u
                dve.wait_ge(delta_ready, n + 1)
                dve.wait_ge(sum_ready, n + 1)
                dve.wait_ge(stored[u], 32 * i)
                st.link(dve.scalar_tensor_tensor(
                    out=x2[u][:].rearrange("p (j c) -> p j c", c=2), in0=pX[u][:].unsqueeze(2).to_broadcast([P, HID, 2]),
                    scalar=0.5, in1=s[u][:].rearrange("p (j c) -> p j c", c=2), op0=ALU.mult, op1=ALU.add))
                st.link(layer_norm(dve, st, z[u][:], x2[u][:], stats[:], mv2[:], norm2, n + 1))
                dve.sem_inc(row_ready, 1)

            def two(i, last):
                front(i, 1)
                back(i, 0)
                if not last:
                    front(i + 1, 0)
                back(i, 1)

            front(0, 0)
            with dve.Fori(0, NT // 2 - 1) as i:
                st.enter(i, 24)
                two(i, False)
            st.leave(NT // 2 - 1)
            two(NT // 2 - 1, True)

        @block.gpsimd
        def _(pool):
            def one(i, u):
                pool.wait_ge(yc_ready, 2 * i + (u + 1))
                if not isinstance(i, int):
                    pool.wait_ge(row_ready, 2 * i + (u - 1))
                pool.tensor_tensor(s[u][:], x1[u][:], y[u][:], ALU.add).then_inc(sum_ready, 1)

            one(0, 0)
            one(0, 1)
            with pool.Fori(1, NT // 2) as i:
                one(i, 0)
                one(i, 1)

        @block.tensor
        def _(pe):
            def one(i, u):
                n = 2 * i + u
                pe.wait_ge(yc_ready, n + 1)
                for c in range(2):
                    last = pe.matmul(pL[u][:, c, :], yc[u][:, c * P:(c + 1) * P], g.pairup[:], start=True, stop=True)
                last.then_inc(low, 1)
                pe.wait_ge(low_copied, n + 1)
                for o in range(2):
                    for c in range(2):
                        last = pe.matmul(pH[u][:, o, :], g.Wf[:, c, o * P:(o + 1) * P], lT[u][:, c, :],
                                         start=(c == 0), stop=(c == 1))
                last.then_inc(hid, 1)
                pe.matmul(pX[u][:], g.unpair[:], yc[u][:], start=True, stop=False)
                pe.matmul(pX[u][:], g.ones[0:1, :], g.fc2b[:], start=False, stop=False)
                pe.wait_ge(hid_done, n + 1)
                for o in range(2):
                    last = pe.matmul(pX[u][:], hT[u][:, o, :], g.fc2T[:, o, :], start=False, stop=(o == 1))
                last.then_inc(delta_ready, 1)

            with pe.Fori(0, NT // 2) as i:
                one(i, 0)
                one(i, 1)

        @block.scalar
        def _(act):
            def mid(i, u):
                n = 2 * i + u
                act.wait_ge(low, n + 1)
                act.activation(lT[u][:], pL[u][:], ACT.Copy).then_inc(low_copied, 1)
                act.wait_ge(hid, n + 1)
                for o in range(2):
                    last = act.activation(hT[u][:, o, :].rearrange("p (i c) -> p i c", c=2),
                                          pH[u][:, o, :].unsqueeze(2).to_broadcast([P, P // 2, 2]),
                                          ACT.Gelu, bias=g.fc1b[:, o:o + 1])
                last.then_inc(hid_done, 1)

            def store(i, u):
                act.wait_ge(row_ready, 2 * i + (u + 1))
                rows = bass.ds((i * 2 + u) * P, P)
                act.dma_start(g.x2[rows, :], x2[u][:]).then_inc(stored[u], 16)
                act.dma_start(g.z[rows, :], z[u][:]).then_inc(stored[u], 16)

            def two(i, last):
                var_root(act, g, mv1, norm1, 2 * i + 2)
                var_root(act, g, mv2, norm2, 2 * i + 1)
                mid(i, 1)
                store(i, 0)
                if not last:
                    var_root(act, g, mv1, norm1, 2 * i + 3)
                var_root(act, g, mv2, norm2, 2 * i + 2)
                if not last:
                    mid(i + 1, 0)
                store(i, 1)

            var_root(act, g, mv1, norm1, 1)
            mid(0, 0)
            with act.Fori(0, NT // 2 - 1) as i:
                two(i, False)
            two(NT // 2 - 1, True)
            for u in range(2):
                act.wait_ge(stored[u], 32 * (NT // 2))


def gin_mlp(nc, g):
    with ExitStack() as ctx:
        sb, sem, ps = g.maker(ctx)
        loaded = sem("m_loaded")
        z_in, x2_in, stored = ([sem(f"m_{n}{u}") for u in range(2)] for n in ("z", "x2", "st"))
        z_free, x2_free, step, h0_ready, h0_turned, h0_copied = (sem(f"m_{n}") for n in (
            "z_free", "x2_free", "step", "h0", "h0t", "h0c"))
        h1_ready, h1_done, o_ready, xb_ready, q_ready, q_turned, q_copied, lg_ready, lg_copied = (
            sem(f"m_{n}") for n in ("h1", "h1d", "o", "xb", "q", "qt", "qc", "lg", "lgc"))
        norm1, norm2 = [sem("m_var1"), sem("m_root1")], [sem("m_var2"), sem("m_root2")]
        W1, W2 = sb("gW1", [P, 4, D]), sb("gW2", [P, 4, D])
        b1, b2, gam, bet = sb("gb1", [P, 4]), sb("gb2", [P, D]), sb("gam", [P, D]), sb("bet", [P, D])
        Wr = sb("gWr", [P, 4, NX])
        zs, x2, xb, x3, q = ([sb(f"m{n}{u}", [P, D]) for u in range(2)] for n in ("zs", "x2", "xb", "x3", "q"))
        h0, o = sb("h0", [P, D]), sb("o", [P, D])
        h0T = [sb(f"h0T{u}", [P, 4, P]) for u in range(2)]
        h1T = [sb(f"h1T{u}", [P, 4, P]) for u in range(2)]
        qT = sb("qT", [P, 4, P])
        lg = [sb(f"lg{u}", [NX, P]) for u in range(2)]
        stats, mv1, mv2 = sb("mstats", [P, 6]), sb("mmv1", [P, 2]), sb("mmv2", [P, 2])
        pT, pQ, pG = ps("mpT", [P, 4, P]), ps("mpQ", [P, 4, P]), ps("mpG", [NX, P])
        pH = [ps(f"mpH{u}", [P, 4, P]) for u in range(2)]
        pO = [ps(f"mpO{u}", [P, D]) for u in range(2)]
        block = ctx.enter_context(nc.Block())

        @block.sync
        def _(sp):
            for w, d in ((W1, g.gW1T), (W2, g.gW2T), (Wr, g.Wr)):
                sp.dma_start(w[:], d.rearrange("(c p) n -> p c n", p=P)).then_inc(loaded, 16)
            sp.dma_start(b1[:], g.gb1).then_inc(loaded, 16)
            for w, d in ((b2, g.gb2), (gam, g.gamma), (bet, g.beta)):
                sp.dma_start(w[:], d.to_broadcast([P, D])).then_inc(loaded, 16)
            with sp.Fori(0, NT // 2) as i:
                for u in range(2):
                    rows = bass.ds((i * 2 + u) * P, P)
                    sp.wait_ge(z_free, 2 * i + (u + 1))
                    sp.dma_start(zs[u][:], g.z[rows, :]).then_inc(z_in[u], 16)
                    sp.wait_ge(x2_free, 2 * i + (u + 1))
                    sp.dma_start(x2[u][:], g.x2[rows, :]).then_inc(x2_in[u], 16)

        @block.gpsimd
        def _(pool):
            pool.sem_inc(x2_free, 2)
            pool.wait_ge(loaded, 16 * 7)

            def one(i, u):
                pool.wait_ge(x2_in[u], 16 * i + 16)
                if not isinstance(i, int):
                    pool.wait_ge(q_ready, 2 * i + (u - 1))
                pool.tensor_tensor(xb[u][:], x2[u][:], bet[:], ALU.add).then_inc(xb_ready, 1)
                pool.wait_ge(xb_ready, 2 * i + (u + 1))
                pool.sem_inc(x2_free, 1)

            one(0, 0)
            one(0, 1)
            with pool.Fori(1, NT // 2) as i:
                one(i, 0)
                one(i, 1)

        @block.vector
        def _(dve):
            st = Steps(dve, step, g)
            dve.sem_inc(z_free, 2)
            dve.wait_ge(loaded, 16 * 7)

            def front(i, u):
                dve.wait_ge(z_in[u], 16 * i + 16)
                dve.wait_ge(h0_turned, 2 * i + u)
                st.link(dve.scalar_tensor_tensor(out=h0[:], in0=zs[u][:], scalar=g.epsb[:, 0:1],
                                                 in1=g.acc[:, bass.ds((2 * i + u) * W, D)], op0=ALU.mult, op1=ALU.add))
                dve.sem_inc(h0_ready, 1)
                dve.sem_inc(z_free, 1)

            def back(i, u):
                n = 2 * i + u
                dve.wait_ge(o_ready, n + 1)
                st.link(dve.tensor_tensor(o[:], pO[u][:], b2[:], ALU.add))
                st.link(layer_norm(dve, st, o[:], o[:], stats[:], mv1[:], norm1, n + 1))
                st.link(dve.tensor_tensor(o[:], o[:], gam[:], ALU.mult))
                dve.wait_ge(xb_ready, n + 1)
                dve.wait_ge(stored[u], 48 * i)
                st.link(dve.tensor_tensor(x3[u][:], o[:], xb[u][:], ALU.add))
                st.link(layer_norm(dve, st, q[u][:], x3[u][:], stats[:], mv2[:], norm2, n + 1))
                dve.sem_inc(q_ready, 1)

            def two(i, last):
                front(i, 1)
                back(i, 0)
                if not last:
                    front(i + 1, 0)
                back(i, 1)

            front(0, 0)
            with dve.Fori(0, NT // 2 - 1) as i:
                st.enter(i, 20)
                two(i, False)
            st.leave(NT // 2 - 1)
            two(NT // 2 - 1, True)

        @block.tensor
        def _(pe):
            pe.wait_ge(loaded, 16 * 7)

            def turn(i, u):
                pe.wait_ge(h0_ready, 2 * i + (u + 1))
                pe.wait_ge(h0_copied, 2 * i + u)
                for c in range(4):
                    last = pe.transpose(pT[:, c, :], h0[:, c * P:(c + 1) * P], g.ident[:])
                last.then_inc(h0_turned, 1)

            def layer1(i, u):
                pe.wait_ge(h0_copied, 2 * i + (u + 1))
                for o_ in range(4):
                    for c in range(4):
                        last = pe.matmul(pH[u][:, o_, :], W1[:, c, o_ * P:(o_ + 1) * P], h0T[u][:, c, :],
                                         start=(c == 0), stop=(c == 3))
                last.then_inc(h1_ready, 1)

            def layer2(i, u):
                pe.wait_ge(h1_done, 2 * i + (u + 1))
                for c in range(4):
                    last = pe.matmul(pO[u][:], h1T[u][:, c, :], W2[:, c, :], start=(c == 0), stop=(c == 3))
                last.then_inc(o_ready, 1)

            def route(i, u):
                pe.wait_ge(q_ready, 2 * i + (u + 1))
                for c in range(4):
                    last = pe.transpose(pQ[:, c, :], q[u][:, c * P:(c + 1) * P], g.ident[:])
                last.then_inc(q_turned, 1)
                pe.wait_ge(q_copied, 2 * i + (u + 1))
                pe.wait_ge(lg_copied, 2 * i + u)
                for c in range(4):
                    last = pe.matmul(pG[:], Wr[:, c, :], qT[:, c, :], start=(c == 0), stop=(c == 3))
                last.then_inc(lg_ready, 1)

            def two(i, last):
                turn(i, 1)
                layer2(i, 0)
                layer1(i, 1)
                route(i, 0)
                if not last:
                    turn(i + 1, 0)
                layer2(i, 1)
                if not last:
                    layer1(i + 1, 0)
                route(i, 1)

            turn(0, 0)
            layer1(0, 0)
            with pe.Fori(0, NT // 2 - 1) as i:
                two(i, False)
            two(NT // 2 - 1, True)

        @block.scalar
        def _(act):
            def copy0(i, u):
                act.wait_ge(h0_turned, 2 * i + (u + 1))
                act.activation(h0T[u][:], pT[:], ACT.Copy).then_inc(h0_copied, 1)

            def relu(i, u):
                act.wait_ge(h1_ready, 2 * i + (u + 1))
                for o_ in range(4):
                    last = act.activation(h1T[u][:, o_, :], pH[u][:, o_, :], ACT.Relu, bias=b1[:, o_:o_ + 1])
                last.then_inc(h1_done, 1)

            def out(i, u):
                n = 2 * i + u
                act.wait_ge(q_ready, n + 1)
                rows = bass.ds((i * 2 + u) * P, P)
                act.dma_start(g.out[rows, :], x3[u][:]).then_inc(stored[u], 16)
                act.dma_start(g.q[rows, :], q[u][:]).then_inc(stored[u], 16)
                act.wait_ge(q_turned, n + 1)
                act.activation(qT[:], pQ[:], ACT.Copy).then_inc(q_copied, 1)
                act.wait_ge(lg_ready, n + 1)
                act.activation(lg[u][:], pG[:], ACT.Copy).then_inc(lg_copied, 1)
                act.wait_ge(lg_copied, n + 1)
                act.dma_start(g.logits[:, rows], lg[u][:]).then_inc(stored[u], 16)

            def two(i, last):
                copy0(i, 1)
                var_root(act, g, mv1, norm1, 2 * i + 1)
                relu(i, 1)
                var_root(act, g, mv2, norm2, 2 * i + 1)
                out(i, 0)
                if not last:
                    copy0(i + 1, 0)
                var_root(act, g, mv1, norm1, 2 * i + 2)
                if not last:
                    relu(i + 1, 0)
                var_root(act, g, mv2, norm2, 2 * i + 2)
                out(i, 1)

            act.wait_ge(loaded, 16 * 7)
            copy0(0, 0)
            relu(0, 0)
            with act.Fori(0, NT // 2 - 1) as i:
                two(i, False)
            two(NT // 2 - 1, True)
            for u in range(2):
                act.wait_ge(stored[u], 48 * (NT // 2))


def choose_tokens(nc, g):
    TB = 5
    NB = NT // TB
    BIS = 40
    with ExitStack() as ctx:
        sb, sem, ps = g.maker(ctx)
        lg_in, masked, lm_out, ls_in, p_io, pos_out, pos_in = (sem(f"r_{n}") for n in (
            "lg_in", "masked", "lm_out", "ls_in", "p_io", "pos_out", "pos_in"))
        step, maxed, exped, normed, lohi, spread, counted, summed = (sem(f"r_{n}") for n in (
            "step", "maxed", "exped", "normed", "lohi", "spread", "counted", "summed"))
        placed, edges, prefixed, turned, hot, packed, tok_ready = (sem(f"r_{n}") for n in (
            "placed", "edges", "prefixed", "turned", "hot", "packed", "tok"))
        A = g.acc
        L8, P8 = A[0:NX, 0:NP], A[0:NX, NP:2 * NP]
        PP = A[0:16, 2 * NP:3 * NP]
        o = 3 * NP
        LS = sb("LS", [P, SEG])
        gt, ge, a, b_, zz = (sb(f"r{n}", [P, SEG]) for n in ("gt", "ge", "a", "b", "zz"))
        mm8, ns8, sum8 = sb("mm8", [NX, 2]), sb("ns8", [NX, 1]), sb("sum8", [NX, 1])
        lh, keep, take, mid, cp = sb("lh", [P, 2]), sb("keep", [P, 2]), sb("take", [P, 2]), sb("mid", [P, 1]), sb("cp", [P, 1])
        c2, off = sb("c2", [P, 2]), sb("off", [P, 2])
        TP = A[:, o:o + NT * 16].rearrange("p (t w) -> p t w", w=16)
        o += NT * 16
        digits_i = A[:, o:o + 2 * NT * NX].bitcast(I32).rearrange("p (d t e) -> p d t e", d=2, e=NX)
        o += 2 * NT * NX
        lo_d = A[:, o:o + NT * NX].rearrange("p (e t) -> p e t", e=NX)
        o += NT * NX
        hi_d = A[:, o:o + NT * NX].rearrange("p (t e) -> p t e", e=NX)
        o += NT * NX
        match = A[:, o:o + NT * NX].rearrange("p (t e) -> p t e", e=NX)
        o += NT * NX
        R = A[:, 0:NX * NT * 8].rearrange("p (e t k) -> p e t k", e=NX, k=8)
        tok = sb("tok", [P, NT])
        hotb = [sb(f"hotb{u}", [P, TB, P]) for u in range(2)]
        pS, pC = ps("rpS", [P, 2]), ps("rpC", [P, 1])
        pP = ps("rpP", [P, 4])
        pT = [ps(f"rpT{u}", [P, NT // 2, 16]) for u in range(2)]
        pK = ps("rpK", [P, NX * 8])
        block = ctx.enter_context(nc.Block())

        @block.sync
        def _(sp):
            sp.dma_start(L8, g.logits).then_inc(lg_in, 16)
            sp.wait_ge(masked, 1)
            sp.dma_start(g.logits_m, L8).then_inc(lm_out, 16)
            sp.wait_ge(lm_out, 16)
            sp.dma_start(LS[:], g.logits_m.rearrange("e (s c) -> (e s) c", s=16)).then_inc(ls_in, 16)
            sp.wait_ge(normed, 1)
            sp.dma_start(g.probs, P8).then_inc(p_io, 16)
            sp.wait_ge(p_io, 16)
            sp.dma_start(PP[NX:2 * NX, :], g.probs).then_inc(p_io, 16)
            sp.wait_ge(placed, 1)
            sp.dma_start(g.places.rearrange("e (s c) -> (e s) c", s=16), b_[:]).then_inc(pos_out, 16)
            sp.wait_ge(pos_out, 16)
            sp.dma_start(PP[0:NX, :], g.places).then_inc(pos_in, 16)
            sp.wait_ge(p_io, 32)
            sp.wait_ge(pos_in, 16)

        @block.gpsimd
        def _(pool):
            pool.iota(tok[:], pattern=[[P, NT]], base=0, channel_multiplier=1,
                      allow_small_or_imprecise_dtypes=True).then_inc(tok_ready, 1)

        @block.scalar
        def _(act):
            act.wait_ge(maxed, 1)
            act.activation(P8, L8, ACT.Exp, bias=ns8[:, 0:1], accum_out=sum8[:, 0:1]).then_inc(exped, 1)

        @block.tensor
        def _(pe):
            pe.wait_ge(lohi, 1)
            pe.matmul(pS[:], g.expand[:], mm8[:], start=True, stop=True).then_inc(spread, 1)
            with pe.Fori(0, BIS) as i:
                pe.wait_ge(counted, i + 1)
                pe.matmul(pC[:], g.group[:], cp[:], start=True, stop=True).then_inc(summed, 1)
            pe.wait_ge(edges, 1)
            pe.matmul(pP[:, 0:2], g.below[:], c2[:], start=True, stop=True)
            pe.matmul(pP[:, 2:4], g.group[:], c2[:], start=True, stop=True).then_inc(prefixed, 1)
            pe.wait_ge(pos_in, 16)
            pe.wait_ge(p_io, 32)
            for t in range(NT):
                last = pe.transpose(pT[t // (NT // 2)][:, t % (NT // 2), :], PP[:, t * P:(t + 1) * P],
                                    g.ident[0:16, 0:16])
            last.then_inc(turned, 1)
            with pe.Fori(0, NX) as e:
                for b in range(NB):
                    pe.wait_ge(hot, NB * e + (b + 1))
                    for t in range(TB):
                        first, end = (b == 0 and t == 0), (b == NB - 1 and t == TB - 1)
                        r = A[:, bass.ds((e * NT + (b * TB + t)) * 8, 8)]
                        last = pe.matmul(pK[:, bass.ds(e * 8, 8)], hotb[b % 2][:, t, :], r, start=first, stop=end)
                    last.then_inc(packed, 1)

        @block.vector
        def _(dve):
            st = Steps(dve, step, g)
            st.mark(dve.memset(zz[:], 0.0))
            dve.wait_ge(lg_in, 16)
            st.link(dve.tensor_reduce(mm8[:, 0:1], L8, AX.X, ALU.min))
            st.mark(dve.tensor_scalar(mm8[:, 0:1], mm8[:, 0:1], -1.0, None, ALU.add))
            st.link(dve.memset(L8[:, N:NP], -1e30))
            dve.sem_inc(masked, 1)
            st.link(dve.tensor_reduce(mm8[:, 1:2], L8, AX.X, ALU.max))
            dve.sem_inc(lohi, 1)
            st.link(dve.tensor_scalar(ns8[:], mm8[:, 1:2], -1.0, None, ALU.mult))
            dve.sem_inc(maxed, 1)
            dve.wait_ge(spread, 1)
            st.link(dve.tensor_copy(lh[:], pS[:]))
            dve.wait_ge(exped, 1)
            st.link(dve.reciprocal(sum8[:], sum8[:]))
            st.link(dve.tensor_scalar(P8, P8, sum8[:, 0:1], None, ALU.mult))
            dve.sem_inc(normed, 1)
            dve.wait_ge(ls_in, 16)
            with dve.Fori(0, BIS) as i:
                st.enter(i, 9)
                st.link(dve.tensor_tensor(mid[:], lh[:, 0:1], lh[:, 1:2], ALU.add))
                st.link(dve.tensor_scalar(mid[:], mid[:], 0.5, None, ALU.mult))
                st.link(dve.tensor_scalar(a[:], LS[:], mid[:, 0:1], 0.0, ALU.is_gt, ALU.add, accum_out=cp[:, 0:1]))
                dve.sem_inc(counted, 1)
                dve.wait_ge(summed, i + 1)
                st.mark(dve.tensor_scalar(take[:, 0:1], pC[:], float(CAP), None, ALU.is_ge))
                st.mark(dve.tensor_scalar(take[:, 1:2], pC[:], float(CAP), None, ALU.is_lt))
                st.mark(dve.tensor_scalar(keep[:, 0:1], pC[:], float(CAP), None, ALU.is_lt))
                st.link(dve.tensor_scalar(keep[:, 1:2], pC[:], float(CAP), None, ALU.is_ge))
                st.link(dve.tensor_tensor(lh[:], lh[:], keep[:], ALU.mult))
                st.link(dve.scalar_tensor_tensor(out=lh[:], in0=take[:], scalar=mid[:, 0:1], in1=lh[:],
                                                 op0=ALU.mult, op1=ALU.add))
            st.leave(BIS)
            st.mark(dve.tensor_scalar(gt[:], LS[:], lh[:, 1:2], None, ALU.is_gt))
            st.link(dve.tensor_scalar(ge[:], LS[:], lh[:, 0:1], None, ALU.is_gt))
            st.link(dve.tensor_tensor(ge[:], ge[:], gt[:], ALU.subtract))
            st.mark(dve.tensor_tensor_scan(a[:], gt[:], zz[:], 0.0, ALU.add, ALU.add))
            st.link(dve.tensor_tensor_scan(b_[:], ge[:], zz[:], 0.0, ALU.add, ALU.add))
            st.mark(dve.tensor_copy(c2[:, 0:1], a[:, SEG - 1:SEG]))
            st.link(dve.tensor_copy(c2[:, 1:2], b_[:, SEG - 1:SEG]))
            dve.sem_inc(edges, 1)
            dve.wait_ge(prefixed, 1)
            st.link(dve.tensor_scalar(off[:], pP[:, 0:2], -1.0, None, ALU.add))
            st.link(dve.tensor_tensor(off[:, 1:2], off[:, 1:2], pP[:, 2:3], ALU.add))
            st.mark(dve.scalar_tensor_tensor(out=a[:], in0=a[:], scalar=off[:, 0:1], in1=gt[:],
                                             op0=ALU.add, op1=ALU.mult))
            st.link(dve.scalar_tensor_tensor(out=b_[:], in0=b_[:], scalar=off[:, 1:2], in1=ge[:],
                                             op0=ALU.add, op1=ALU.mult))
            st.link(dve.tensor_tensor(b_[:], b_[:], a[:], ALU.add))
            st.link(dve.tensor_scalar(a[:], LS[:], lh[:, 0:1], 9999.0, ALU.is_le, ALU.mult))
            st.link(dve.tensor_tensor(b_[:], b_[:], a[:], ALU.add))
            dve.sem_inc(placed, 1)
            dve.wait_ge(turned, 1)
            half = NT // 2
            st.mark(dve.tensor_copy(TP[:, 0:half, :], pT[0][:]))
            st.link(dve.tensor_copy(TP[:, half:NT, :], pT[1][:]))
            st.link(dve.tensor_copy(digits_i[:, 0, :, :], TP[:, :, 0:NX]))
            st.link(dve.tensor_scalar(digits_i[:, 1, :, :], digits_i[:, 0, :, :], 7, None, ALU.logical_shift_right))
            st.link(dve.tensor_scalar(digits_i[:, 0, :, :], digits_i[:, 0, :, :], P - 1, None, ALU.bitwise_and))
            st.mark(dve.tensor_copy(lo_d.rearrange("p e t -> p t e"), digits_i[:, 0, :, :]))
            st.link(dve.tensor_copy(hi_d, digits_i[:, 1, :, :]))
            dve.wait_ge(tok_ready, 1)
            dve.wait_ge(p_io, 32)
            for c in range(CAP // P):
                st.link(dve.tensor_scalar(match, hi_d, float(c), None, ALU.is_equal))
                st.mark(dve.tensor_tensor(R[:, :, :, c].rearrange("p e t -> p t e"), match,
                                          tok[:].unsqueeze(2).to_broadcast([P, NT, NX]), ALU.mult))
                st.link(dve.tensor_tensor(R[:, :, :, 4 + c].rearrange("p e t -> p t e"), match,
                                          TP[:, :, NX:2 * NX], ALU.mult))

            def batch(e, b):
                k = lo_d.rearrange("p e t -> p (e t)")[:, bass.ds(e * NT + b * TB, TB)]
                dve.tensor_tensor(hotb[b % 2][:], g.iota[:].unsqueeze(1).to_broadcast([P, TB, P]),
                                  k.unsqueeze(2).to_broadcast([P, TB, P]), ALU.is_equal).then_inc(hot, 1)

            for b in range(NB):
                if b >= 2:
                    dve.wait_ge(packed, b - 1)
                batch(0, b)
            with dve.Fori(1, NX) as e:
                for b in range(NB):
                    dve.wait_ge(packed, NB * e + (b - 1))
                    batch(e, b)
            dve.wait_ge(packed, NX * NB)
            k = pK[:].rearrange("p (e w c) -> p e w c", e=NX, w=2)
            st.mark(dve.tensor_copy(g.tok_i[:].rearrange("p (e c) -> p e c", e=NX), k[:, :, 0, :]))
            st.link(dve.tensor_copy(g.tok_p[:].rearrange("p (e c) -> p e c", e=NX), k[:, :, 1, :]))


def experts(nc, g):
    NC = CAP // P
    with ExitStack() as ctx:
        sb, sem, ps = g.maker(ctx)
        w_in, x_in, added = [sem(f"f_w{u}") for u in range(2)], g.sw["x_in"], g.sw["added"][0]
        staged, y_free, w_free, x_turned, x_copied, h_ready, h_done, y_ready, y_done, step = (sem(f"f_{n}") for n in (
            "staged", "y_free", "w_free", "xt", "xc", "h", "hd", "y", "yd", "step"))
        w1, w2, b1, b2 = ([sb(f"f{n}{u}", s) for u in range(2)] for n, s in (
            ("w1", [P, 4, FX]), ("w2", [P, 2, D]), ("b1", [P, 2]), ("b2", [P, D])))
        o = 0

        def arena(n):
            nonlocal o
            o += n
            return g.acc[:, o - n:o]

        X = [arena(NC * D).rearrange("p (c n) -> p c n", c=NC) for u in range(2)]
        Y = [arena(NC * D).rearrange("p (c n) -> p c n", c=NC) for u in range(2)]
        XT = arena(4 * CAP).rearrange("p (c n) -> p c n", c=4)
        HT = arena(2 * CAP).rearrange("p (c n) -> p c n", c=2)
        st_i = [sb(f"fi{u}", [P, NC], I32) for u in range(2)]
        pT = [ps(f"fT{u}", [P, CAP]) for u in range(2)]
        pH = [ps(f"fH{u}", [P, CAP]) for u in range(2)]
        pY = [ps(f"fY{u}", [P, D]) for u in range(2)]
        block = ctx.enter_context(nc.Block())

        @block.sync
        def _(sp):
            with sp.Fori(0, NX // 2) as i:
                for u in range(2):
                    e = i * 2 + u
                    sp.wait_ge(w_free, 2 * i + (u + 1))
                    sp.dma_start(w1[u][:], g.eW1[bass.ds(e * D, D), :].rearrange("(c p) n -> p c n", p=P))\
                      .then_inc(w_in[u], 16)
                    sp.dma_start(w2[u][:], g.eW2[bass.ds(e * FX, FX), :].rearrange("(c p) n -> p c n", p=P))\
                      .then_inc(w_in[u], 16)
                    sp.dma_start(b1[u][:], g.eb1[bass.ds(e * P, P), :]).then_inc(w_in[u], 16)
                    sp.dma_start(b2[u][:], g.eb2[bass.ds(e, 1), :].to_broadcast([P, D])).then_inc(w_in[u], 16)

        @block.gpsimd
        def _(pool):
            def gather(i, u):
                pool.tensor_copy(st_i[u][:], g.tok_i[:, bass.ds((2 * i + u) * NC, NC)]).then_inc(staged, 1)
                wait_apart(pool, g, staged, 2 * i + (u + 1))
                for c in range(NC):
                    pool.indirect_dma_start(X[u][:, c, :], None, g.q,
                                            bass.IndirectOffsetOnAxis(ap=st_i[u][:, c:c + 1], axis=0))\
                        .then_inc(x_in[u], 16)

            def scatter(i, u):
                wait_apart(pool, g, y_done, (2 * i + u) * NC + NC)
                for c in range(NC):
                    pool.indirect_dma_start(g.out, bass.IndirectOffsetOnAxis(ap=st_i[u][:, c:c + 1], axis=0),
                                            Y[u][:, c, :], None, compute_op=ALU.add).then_inc(added, 16)
                pool.wait_ge(added, (2 * i + (u + 1)) * (16 * NC))
                pool.sem_inc(y_free, 1)

            pool.sem_inc(y_free, 2)
            gather(0, 0)
            with pool.Fori(0, NX // 2 - 1) as i:
                gather(i, 1)
                scatter(i, 0)
                gather(i + 1, 0)
                scatter(i, 1)
            gather(NX // 2 - 1, 1)
            scatter(NX // 2 - 1, 0)
            scatter(NX // 2 - 1, 1)

        @block.tensor
        def _(pe):
            with pe.Fori(0, NX // 2) as i:
                for u in range(2):
                    e = 2 * i + u
                    pe.wait_ge(x_in[u], (16 * NC) * i + 16 * NC)
                    for c in range(4):
                        if c >= 2:
                            pe.wait_ge(x_copied, e * 4 + (c - 1))
                        for t in range(NC):
                            last = pe.transpose(pT[c % 2][:, t * P:(t + 1) * P], X[u][:, t, c * P:(c + 1) * P], g.ident[:])
                        last.then_inc(x_turned, 1)
                    pe.wait_ge(x_copied, e * 4 + 4)
                    pe.wait_ge(w_in[u], 64 * i + 64)
                    for f in range(2):
                        for c in range(4):
                            last = pe.matmul(pH[f][:], w1[u][:, c, f * P:(f + 1) * P], XT[:, c, :],
                                             start=(c == 0), stop=(c == 3))
                        last.then_inc(h_ready, 1)
                    pe.wait_ge(h_done, 2 * e + 2)
                    for t in range(NC):
                        pe.wait_ge(y_done, e * NC + max(t - 1, 0))
                        for f in range(2):
                            last = pe.matmul(pY[t % 2][:], HT[:, f, t * P:(t + 1) * P], w2[u][:, f, :],
                                             start=(f == 0), stop=(f == 1))
                        last.then_inc(y_ready, 1)

        @block.scalar
        def _(act):
            with act.Fori(0, NX // 2) as i:
                for u in range(2):
                    e = 2 * i + u
                    for c in range(4):
                        act.wait_ge(x_turned, e * 4 + (c + 1))
                        act.activation(XT[:, c, :], pT[c % 2][:], ACT.Copy).then_inc(x_copied, 1)
                    act.wait_ge(w_in[u], 64 * i + 64)
                    for f in range(2):
                        act.wait_ge(h_ready, e * 2 + (f + 1))
                        act.wait_ge(y_ready, e * NC)
                        act.activation(HT[:, f, :], pH[f][:], ACT.Gelu, bias=b1[u][:, f:f + 1]).then_inc(h_done, 1)

        @block.vector
        def _(dve):
            dve.sem_inc(w_free, 2)
            with dve.Fori(0, NX // 2) as i:
                for u in range(2):
                    e = 2 * i + u
                    dve.wait_ge(w_in[u], 64 * i + 64)
                    dve.wait_ge(y_free, 2 * i + (u + 1))
                    for t in range(NC):
                        dve.wait_ge(y_ready, e * NC + (t + 1))
                        y = Y[u][:, t, :]
                        dve.tensor_tensor(y, pY[t % 2][:], b2[u][:], ALU.add).then_inc(step, 1)
                        dve.wait_ge(step, e * NC + (t + 1))
                        dve.tensor_scalar(y, y, g.tok_p[:, bass.ds(e * NC + t, 1)], None, ALU.mult).then_inc(y_done, 1)
                    dve.wait_ge(y_done, e * NC + NC)
                    dve.sem_inc(w_free, 1)


class Shared:
    pass


def build(nc, x, src, dst, W_src, b_src, W_dst, b_dst, W_val, b_val, attn_l, attn_r, fc1T, fc1_b, fc2T, fc2_b,
          eps, gW1T, gb1, gW2T, gb2, gamma, beta, Wr, eW1, eb1, eW2, eb2, interp, out):
    g = Shared()
    row = lambda v: v.unsqueeze(0)
    g.x, g.src, g.dst, g.W_src, g.W_dst, g.W_val, g.fc1T, g.fc2T_d = x, src, dst, W_src, W_dst, W_val, fc1T, fc2T
    g.b_src, g.b_dst, g.b_val, g.attn_l, g.attn_r = row(b_src), row(b_dst), row(b_val), row(attn_l), row(attn_r)
    g.fc1_b, g.fc2_b, g.eps = fc1_b, row(fc2_b), row(eps)
    g.gW1T, g.gb1, g.gW2T, g.gb2, g.gamma, g.beta, g.Wr = gW1T, gb1, gW2T, row(gb2), row(gamma), row(beta), Wr
    g.eW1, g.eb1, g.eW2, g.eb2, g.interp, g.out = eW1, eb1, eW2, eb2, interp, out

    def dram(name, shape, dt=F32):
        return nc.dram_tensor(name, shape, dt, kind="Internal").ap()

    g.by_src = dram("by_src", [WL * PAIR, 2], I32)
    g.tiles_d = dram("tiles_d", [2, WL], I32)
    g.ve, g.x2, g.z, g.q = dram("ve", [NP, W]), dram("x2_d", [NP, D]), dram("z_d", [NP, D]), dram("q_d", [NP, D])
    g.logits, g.logits_m, g.probs, g.places = (dram(n, [NX, NP]) for n in ("lg_d", "lgm_d", "pr_d", "pos_d"))

    with ExitStack() as ctx:
        def maker(c):
            sems = []

            def clear():
                if sems:
                    for n in sems:
                        nc.gpsimd.sem_clear(n)
                    nc.all_engine_barrier()

            c.callback(clear)

            def sb(name, shape, dt=F32):
                return c.enter_context(nc.sbuf_tensor(name, shape, dt))

            def sem(name):
                sems.append(c.enter_context(nc.semaphore(name)))
                return sems[-1]

            def ps(name, shape):
                n = int(np.prod(shape[1:]))
                t = c.enter_context(nc.psum_tensor(name, [shape[0], 512], F32))
                v = t[:][:, 0:n]
                if len(shape) > 2:
                    names = "abc"[:len(shape) - 1]
                    v = v.rearrange(f"p ({' '.join(names)}) -> p {' '.join(names)}",
                                    **{m: k for m, k in zip(names, shape[1:])})
                return v
            return sb, sem, ps

        g.maker = maker
        sb, new_sem, _ = maker(ctx)
        g.passed = new_sem("passed")
        g.sw = {n: [new_sem(f"sw_{n}{u}") for u in range(k)] for n, k in (
            ("rows", 1), ("scattered", 2), ("got0", 4 * QI), ("got1", 4 * QI), ("x_in", 2), ("added", 1))}
        g.acc = sb("acc", [P, NT * W])[:]
        g.ident, g.ones, g.upper, g.group, g.below, g.unpair, g.iota = (sb(n, [P, P]) for n in (
            "ident", "ones", "upper", "group", "below", "unpair", "iota"))
        g.pairup, g.expand = sb("pairup", [P, P // 2]), sb("expand", [NX, P])
        g.Wv, g.Wlr, g.bv, g.blr = sb("Wv", [P, 4, D]), sb("Wlr", [P, 4, 2 * H]), sb("bv", [P, D]), sb("blr", [P, 2 * H])
        g.Wf, g.fc1b, g.fc2T, g.fc2b = sb("Wf", [P, 2, HID]), sb("fc1b", [P, 2]), sb("fc2T", [P, 2, HID]), sb("fc2b", [1, HID])
        g.epsb, g.ln_eps = sb("epsb", [P, 1]), sb("ln_eps", [P, 1])
        g.erm = sb("erm", [P, NT * 2 * H])
        g.tile_base = sb("tile_base", [P, 2, 4])
        g.tiles = sb("tiles", [1, 2 * WL], I32)
        g.idx, g.key = sb("idx", [P, 2 * WL], I32), sb("key", [P, 2 * WL])
        g.tok_i, g.tok_p = sb("tok_i", [P, NX * 4], I32), sb("tok_p", [P, NX * 4])
        fold_consts(nc, g)
        with ExitStack() as early:
            esb, _, _ = maker(early)
            g.rec, g.place = esb("rec", [P, EC, 2], I32), esb("place", [P, EC], I32)
            g.rows = esb("rows", [P, 4, 2, PAIR], I32)
            plan_edges(nc, g)
            build_index(nc, g, 0)
            project(nc, g)
        edge_pass(nc, g, 0)
        wavelet_ffn(nc, g)
        with ExitStack() as mid:
            g.rows = maker(mid)[0]("rows1", [P, 4, 2, PAIR], I32)
            build_index(nc, g, 1)
        edge_pass(nc, g, 1)
        gin_mlp(nc, g)
        choose_tokens(nc, g)
        experts(nc, g)


def interpolation():
    n, m = D // 2, D
    pos = np.linspace(0.0, 1.0, m, dtype=np.float32) * np.float32(n - 1)
    i0 = np.clip(np.floor(pos).astype(np.int32), 0, n - 2)
    w = pos - i0.astype(np.float32)
    u = np.zeros((n, m), np.float32)
    u[i0, np.arange(m)] = np.float32(1.0) - w
    u[i0 + 1, np.arange(m)] += w
    return u


def layout(a):
    c = np.ascontiguousarray
    a = {k: np.asarray(v) for k, v in a.items()}
    pad = np.full(EP - NE, PAD_NODE, np.int32)
    m = {
        "x": np.concatenate([a["x"], np.zeros((NP - N, D), np.float32)]),
        "src": np.concatenate([a["src"], pad]), "dst": np.concatenate([a["dst"], pad]),
        "W_src": a["L0_gnn_W_src"], "b_src": a["L0_gnn_b_src"], "W_dst": a["L0_gnn_W_dst"],
        "b_dst": a["L0_gnn_b_dst"], "W_val": a["L0_gnn_W_val"], "b_val": a["L0_gnn_b_val"],
        "attn_l": a["L0_gnn_attn_l"].reshape(-1), "attn_r": a["L0_gnn_attn_r"].reshape(-1),
        "fc1T": a["L0_ffn_fc1_w"].T, "fc1_b": a["L0_ffn_fc1_b"].reshape(2, P).T, "fc2T": a["L0_ffn_fc2_w"].T,
        "fc2_b": a["L0_ffn_fc2_b"], "eps": a["L1_gnn_eps"].reshape(1), "gW1T": a["L1_gnn_W1"].T,
        "gb1": a["L1_gnn_b1"].reshape(4, P).T, "gW2T": a["L1_gnn_W2"].T, "gb2": a["L1_gnn_b2"], "gamma": a["L1_gnn_gamma"],
        "beta": a["L1_gnn_beta"], "Wr": a["L1_ffn_Wr"], "eW1": a["L1_ffn_W1"].reshape(NX * D, FX),
        "eb1": a["L1_ffn_b1"].reshape(NX, 2, P).transpose(0, 2, 1).reshape(NX * P, 2), "eW2": a["L1_ffn_W2"].reshape(NX * FX, D),
        "eb2": a["L1_ffn_b2"], "interp": c(interpolation().T),
    }
    return {k: c(v) for k, v in m.items()}


def kernel(**inputs):
    import concourse.bacc as bacc
    from concourse.bass_utils import run_bass_kernel_spmd

    arrays = layout(inputs)
    nc = bacc.Bacc("TRN2", target_bir_lowering=False, num_devices=1)
    aps = [nc.dram_tensor("in_" + k, v.shape, mybir.dt.from_np(v.dtype), kind="ExternalInput").ap()
           for k, v in arrays.items()]
    aps.append(nc.dram_tensor("out_nodes", (NP, D), F32, kind="ExternalOutput").ap())
    build(nc, *aps)
    r = run_bass_kernel_spmd(nc, [{"in_" + k: v for k, v in arrays.items()}], core_ids=[0])
    return r.results[0]["out_nodes"][:N]
```

```python
from contextlib import ExitStack

import numpy as np
import concourse.bass as bass
import concourse.mybir as mybir

ALU = mybir.AluOpType
ACT = mybir.ActivationFunctionType
F32 = mybir.dt.float32
I32 = mybir.dt.int32
I16 = mybir.dt.int16
BF16 = mybir.dt.bfloat16
AX = mybir.AxisListType

P = 128
N, D, H = 6250, 512, 8
F = D // H
NT = 50
NP = NT * P
T = -(-N // P)
NE = 100000
EC = 784
EP = P * EC
PAIR = 2 * P
ROWS = EP // PAIR
PAD_NODE = T * P - 1
NPAIR = 440
QN = NPAIR // 2
QI = 4
ITER = QN // QI
WL = 512
W = D + H
EPS = 1e-5
FAR = 30000
HID = 256
NX, FX, CAP = 8, 256, 512
SEG = NP // 16
SCAT = ((12, 11), (ITER, 2), (NT // 2, 6))
assert T % 8 == 1
assert 2 * SCAT[0][0] * SCAT[0][1] <= EC // 2
assert 2 * sum(n * c for n, c in SCAT) == EC and 4 * (T // 4) == T - 1
assert ROWS + T - 1 <= NPAIR and ITER * QI * 2 == NPAIR


class Steps:

    def __init__(self, eng, sem, g=None):
        self.g = g
        self.eng, self.sem, self.base, self.k, self.i, self.per = eng, sem, 0, 0, None, 0

    def value(self):
        return self.base + self.k if self.i is None else self.i * self.per + (self.base + self.k)

    def mark(self, ins):
        self.k += 1
        ins.then_inc(self.sem, 1)
        return self.value()

    def link(self, ins):
        self.mark(ins)
        self.eng.wait_ge(self.sem, self.value())

    def enter(self, i, per):
        self.base, self.k, self.i, self.per = self.base + self.k, 0, i, per

    def leave(self, n):
        assert self.k == self.per, (self.k, self.per)
        self.base, self.k, self.i = self.base + self.per * n, 0, None


def fold_consts(nc, g):
    with ExitStack() as ctx:
        sb, sem, ps = g.maker(ctx)
        loaded, pool_done, dve_done, fold_ready = sem("c_loaded"), sem("c_pool"), sem("c_dve"), sem("c_fold")
        w_raw = g.acc[:, 0:2048].rearrange("p (c n) -> p c n", c=4)
        w_tmp = g.acc[:, 2048:4096].rearrange("p (c n) -> p c n", c=4)
        att = sb("att", [P, 2 * D])
        brow = sb("brow", [P, 2 * D])
        ut = g.acc[:, 4096:5120].rearrange("p (c n) -> p c n", c=4)
        f1 = g.acc[:, 5120:6144].rearrange("p (c n) -> p c n", c=4)
        pw = ps("pw", [P, 2, HID])
        w_dst_raw = g.acc[:, 6144:8192].rearrange("p (c n) -> p c n", c=4)
        block = ctx.enter_context(nc.Block())

        @block.sync
        def _(sp):
            sp.dma_start(w_raw, g.W_src.rearrange("(c p) n -> p c n", p=P)).then_inc(loaded, 16)
            sp.dma_start(w_dst_raw, g.W_dst.rearrange("(c p) n -> p c n", p=P)).then_inc(loaded, 16)
            for j, (a, b) in enumerate(((g.attn_l, g.b_src), (g.attn_r, g.b_dst))):
                sp.dma_start(att[:, j * D:(j + 1) * D], a.to_broadcast([P, D])).then_inc(loaded, 16)
                sp.dma_start(brow[:, j * D:(j + 1) * D], b.to_broadcast([P, D])).then_inc(loaded, 16)
            sp.dma_start(ut, g.interp.rearrange("(c p) n -> p c n", p=P)).then_inc(loaded, 16)
            sp.dma_start(f1, g.fc1T.rearrange("(c p) n -> p c n", p=P)).then_inc(loaded, 16)
            sp.dma_start(g.fc1b[:], g.fc1_b).then_inc(loaded, 16)
            sp.dma_start(g.fc2T[:], g.fc2T_d.rearrange("(c p) n -> p c n", p=P)).then_inc(loaded, 16)
            sp.dma_start(g.fc2b[:], g.fc2_b).then_inc(loaded, 16)
            sp.dma_start(g.Wv[:, :, 0:D], g.W_val.rearrange("(c p) n -> p c n", p=P)).then_inc(loaded, 16)
            sp.dma_start(g.bv[:, 0:D], g.b_val.to_broadcast([P, D])).then_inc(loaded, 16)
            sp.dma_start(g.epsb[:], g.eps.to_broadcast([P, 1])).then_inc(loaded, 16)
            sp.wait_ge(loaded, 16 * 14)

        @block.gpsimd
        def _(pool):
            st = Steps(pool, pool_done)
            st.mark(pool.memset(g.ident[:], 0.0))
            st.mark(pool.memset(g.ones[:], 1.0))
            st.mark(pool.memset(g.ln_eps[:], EPS))
            st.mark(pool.memset(g.upper[:], 1.0))
            st.mark(pool.memset(g.pairup[:], 0.5))
            st.mark(pool.iota(g.iota[:], pattern=[[1, P]], base=0, channel_multiplier=0,
                              allow_small_or_imprecise_dtypes=True))
            pool.wait_ge(pool_done, st.value())
            st.mark(pool.affine_select(out=g.ident[:], in_=g.ident[:], compare_op=ALU.not_equal, fill=1.0, base=0,
                                       pattern=[[-1, P]], channel_multiplier=1))
            st.mark(pool.affine_select(out=g.upper[:], in_=g.upper[:], compare_op=ALU.is_gt, fill=0.0, base=0,
                                       pattern=[[1, P]], channel_multiplier=-1))
            v = g.pairup[:]
            st.link(pool.affine_select(out=v, in_=v, compare_op=ALU.is_ge, fill=0.0, base=0,
                                       pattern=[[-2, P // 2]], channel_multiplier=1))
            st.mark(pool.affine_select(out=v, in_=v, compare_op=ALU.is_ge, fill=0.0, base=1,
                                       pattern=[[2, P // 2]], channel_multiplier=-1))

        @block.vector
        def _(dve):
            st = Steps(dve, dve_done)
            dve.wait_ge(loaded, 16 * 14)
            for j, w in enumerate((w_raw, w_dst_raw)):
                a = att[:, j * D:(j + 1) * D].unsqueeze(1).to_broadcast([P, 4, D])
                st.link(dve.tensor_tensor(w_tmp, w, a, ALU.mult))
                st.link(dve.tensor_reduce(g.Wlr[:, :, j * H:(j + 1) * H],
                                          w_tmp.rearrange("p c (h f) -> p c h f", h=H), AX.X, ALU.add))
                b = brow[:, j * D:(j + 1) * D]
                st.link(dve.tensor_tensor(b, b, att[:, j * D:(j + 1) * D], ALU.mult))
                st.link(dve.tensor_reduce(g.blr[:, j * H:(j + 1) * H],
                                          b.rearrange("p (h f) -> p h f", h=H), AX.X, ALU.add))
            dve.wait_ge(pool_done, 10)
            v = g.unpair[:].rearrange("p (a b) -> p a b", b=2)
            st.link(dve.tensor_scalar(v, g.pairup[:].unsqueeze(2).to_broadcast([P, P // 2, 2]), -1.0, None, ALU.mult))
            st.link(dve.tensor_scalar(g.epsb[:], g.epsb[:], 1.0, None, ALU.add))
            dve.wait_ge(fold_ready, 1)
            st.link(dve.tensor_copy(g.Wf[:], pw[:]))

        @block.tensor
        def _(pe):
            pe.wait_ge(loaded, 16 * 14)
            for jb in range(2):
                for c in range(4):
                    last = pe.matmul(pw[:, jb, :], ut[:, c, jb * P:(jb + 1) * P], f1[:, c, :],
                                     start=(c == 0), stop=(c == 3))
            last.then_inc(fold_ready, 1)


def plan_edges(nc, g):
    TU = 7
    assert T % TU == 0
    with ExitStack() as ctx:
        sb, sem, ps = g.maker(ctx)
        loaded, step, filled, prefilled = sem("p_loaded"), sem("p_step"), sem("p_filled"), sem("p_prefilled")
        counted, summed = sem("p_counted"), sem("p_summed")
        tiles_out, planned, tiles_in = sem("p_tiles_out"), sem("p_planned"), sem("p_tiles_in")
        pool_io, rows_in = sem("p_pool_io"), g.sw["rows"][0]
        A = g.acc
        src_i, dst_i = A[:, 0:EC].bitcast(I32), A[:, EC:2 * EC].bitcast(I32)
        hs, hd = (A[:, k * EC:(k + 1) * EC].bitcast(BF16)[:, 0:EC] for k in (4, 5))
        junk_s, junk_d = (A[:, k * EC:(k + 1) * EC].bitcast(BF16)[:, 0:EC] for k in (2, 3))
        hi_s, hi_d = A[:, 6 * EC:7 * EC].bitcast(I32), A[:, 7 * EC:8 * EC].bitcast(I32)
        zeros = A[:, 10 * EC:11 * EC]
        fill = A[:, 12 * EC:12 * EC + 2048].bitcast(I32)
        g.src_tile, g.zeros = hs, zeros
        cnt = sb("cnt", [P, 2 * T])
        tot = sb("tot", [P, 2 * T])
        base, tiota = g.bucket_base, g.tiota
        s = [sb(f"pl{i}", [P, T]) for i in range(8)]
        si = sb("pli", [P, T], I32)
        kcol = sb("kcol", [P, 4])
        tk = sb("tk", [P, 2, 4])
        tki = sb("tki", [P, 2, 4], I32)
        rowf = sb("rowf", [P, 4])
        rowi = sb("rowi", [P, 4], I32)
        junk = sb("junk", [P, T])
        pt = ps("pt", [P, 2 * T])
        pb = ps("pb", [P, T])
        block = ctx.enter_context(nc.Block())

        @block.sync
        def _(sp):
            sp.dma_start(src_i, g.src.rearrange("(p c) -> p c", p=P)).then_inc(loaded, 16)
            sp.dma_start(dst_i, g.dst.rearrange("(p c) -> p c", p=P)).then_inc(loaded, 16)
            sp.wait_ge(filled, 1)
            sp.dma_start(g.by_src.rearrange("(p k) c -> p (k c)", p=P), fill).then_inc(prefilled, 16)
            sp.wait_ge(planned, 1)
            for layer in range(2):
                sp.dma_start(g.tiles_d[layer, :].rearrange("(p b) -> p b", p=P), tki[:, layer, :])\
                  .then_inc(tiles_out, 16)
            sp.wait_ge(tiles_out, 32)
            sp.dma_start(g.tiles[:], g.tiles_d.rearrange("a k -> (a k)").unsqueeze(0)).then_inc(tiles_in, 16)
            sp.wait_ge(tiles_in, 16)
            sp.wait_ge(prefilled, 16)

        @block.gpsimd
        def _(pool):
            st = Steps(pool, pool_io)
            st.mark(pool.iota(tiota[:], pattern=[[1, T]], base=0, channel_multiplier=0,
                              allow_small_or_imprecise_dtypes=True))
            st.mark(pool.iota(kcol[:], pattern=[[1, 4]], base=0, channel_multiplier=4,
                              allow_small_or_imprecise_dtypes=True))
            f = fill.rearrange("p (k c) -> p k c", c=2)
            pool.memset(f[:, :, 1], 0)
            pool.memset(f[:, :, 0], FAR).then_inc(filled, 1)
            st.mark(pool.memset(zeros, 0.0))
            pool.wait_ge(loaded, 32)
            r = g.rec
            pool.tensor_copy(r[:, :, 0], src_i)
            st.mark(pool.tensor_copy(r[:, :, 1], dst_i))
            pool.wait_ge(planned, 1)
            for arr, out in ((g.src, g.rows[:, :, 0]), (g.dst, g.rows[:, :, 1])):
                for b in range(4):
                    pool.indirect_dma_start(out[:, b, :], None, arr.rearrange("(r e) -> r e", e=PAIR),
                                            bass.IndirectOffsetOnAxis(ap=rowi[:, b:b + 1], axis=0))\
                        .then_inc(rows_in, 16)
            pool.wait_ge(rows_in, 16 * 8)

        @block.tensor
        def _(pe):
            pe.wait_ge(counted, 1)
            pe.matmul(pt[:], g.ones[:], cnt[:], start=True, stop=True)
            pe.matmul(pb[:], g.upper[:], cnt[:, 0:T], start=True, stop=True).then_inc(summed, 1)

        @block.vector
        def _(dve):
            st = Steps(dve, step, g)
            dve.wait_ge(loaded, 32)
            dve.wait_ge(pool_io, 4)
            st.mark(dve.tensor_scalar(hi_s, src_i, 7, None, ALU.logical_shift_right))
            st.link(dve.tensor_scalar(hi_d, dst_i, 7, None, ALU.logical_shift_right))
            st.mark(dve.tensor_copy(hs, hi_s))
            st.link(dve.tensor_copy(hd, hi_d))
            with dve.Fori(0, T // TU) as i:
                st.enter(i, 2 * TU)
                for j in range(TU):
                    b = i * TU + j
                    for h, out, o in ((hs, junk_s, 0), (hd, junk_d, T)):
                        dve.wait_ge(step, st.value() - 1)
                        st.mark(dve.tensor_scalar(out, h, tiota[:, bass.ds(b, 1)], 0.0, ALU.is_equal, ALU.add,
                                                  accum_out=cnt[:, bass.ds(b + o, 1)]))
            st.leave(T // TU)
            dve.wait_ge(step, st.value())
            dve.sem_inc(counted, 1)
            dve.wait_ge(summed, 1)
            st.mark(dve.tensor_copy(tot[:], pt[:]))
            st.link(dve.tensor_copy(base[:], pb[:]))
            z = zeros[:, 0:T]

            def shift(out, x, add):
                st.link(dve.tensor_scalar(out, x, float(add), None, ALU.add))
                st.link(dve.tensor_copy(si[:], out))
                st.link(dve.tensor_scalar(si[:], si[:], 8, None, ALU.logical_shift_right))
                st.link(dve.tensor_copy(out, si[:]))

            n1, end1, n0, end0, first, a, d0, dd = (x[:] for x in s)
            shift(n1, tot[:, 0:T], PAIR - 1)
            st.link(dve.tensor_tensor_scan(end1, n1, z, 0.0, ALU.add, ALU.add))
            st.link(dve.tensor_tensor(a, end1, n1, ALU.subtract))
            st.link(dve.tensor_scalar(a, a, float(PAIR), -1.0, ALU.mult, ALU.add))
            st.link(dve.tensor_tensor(base[:], base[:], a, ALU.add))
            te = tot[:, T:2 * T]
            st.link(dve.tensor_tensor_scan(end0, te, z, 0.0, ALU.add, ALU.add))
            st.link(dve.tensor_tensor(a, end0, te, ALU.subtract))
            st.link(dve.tensor_scalar(n0, a, 1.0, None, ALU.add))
            shift(first, a, 0)
            st.link(dve.tensor_tensor(a, end0, n0, ALU.max))
            shift(n0, a, -1)
            st.link(dve.tensor_tensor(n0, n0, first, ALU.subtract))
            st.link(dve.tensor_scalar(n0, n0, 1.0, None, ALU.add))
            st.link(dve.tensor_tensor_scan(end0, n0, z, 0.0, ALU.add, ALU.add))
            st.link(dve.tensor_tensor(d0, end0, n0, ALU.subtract))
            st.link(dve.tensor_tensor(d0, first, d0, ALU.subtract))
            st.link(dve.memset(dd, 0.0))
            st.link(dve.tensor_tensor(dd[:, 0:T - 1], d0[:, 1:T], d0[:, 0:T - 1], ALU.subtract))
            for b in range(4):
                k = kcol[:, b:b + 1]
                for layer, end in ((0, end0), (1, end1)):
                    st.link(dve.tensor_scalar(junk[:], end, k, 0.0, ALU.is_le, ALU.add,
                                              accum_out=tk[:, layer, b:b + 1]))
                    if layer == 0:
                        st.link(dve.tensor_tensor_reduce(out=junk[:], in0=junk[:], in1=dd, scale=1.0, scalar=0.0,
                                                         op0=ALU.mult, op1=ALU.add, accum_out=rowf[:, b:b + 1]))
            st.link(dve.tensor_tensor(rowf[:], rowf[:], kcol[:], ALU.add))
            st.link(dve.tensor_scalar(rowf[:], rowf[:], d0[:, 0:1], float(ROWS - 1), ALU.add, ALU.min))
            st.link(dve.tensor_copy(rowi[:], rowf[:]))
            st.link(dve.tensor_scalar(g.tile_base[:], tk[:], float(P), None, ALU.mult))
            st.link(dve.tensor_scalar(tk[:], tk[:], float(T - 1), None, ALU.min))
            st.link(dve.tensor_copy(tki[:], tk[:]))
            dve.sem_inc(planned, 1)


def scatter_records(pool, g, phase, i, u):
    done = sum(n * c for n, c in SCAT[:phase])
    turns = sum(n for n, c in SCAT[:phase])
    c = SCAT[phase][1]
    first = phase == 0 and isinstance(i, int) and i == 0
    if not first:
        pool.wait_ge(g.sw["scattered"][u], i * (16 * c) + 16 * done)
    col = i * (2 * c) + (2 * done + u * c)
    pool.tensor_copy(g.place_st[u][:, 0:c], g.place[:, bass.ds(col, c)]).then_inc(g.sc_staged, 1)
    pool.tensor_copy(g.rec_st[u][:, 0:c, :], g.rec[:, bass.ds(col, c), :]).then_inc(g.sc_staged, 1)
    wait_apart(pool, g, g.sc_staged, 4 * i + (4 * turns + 2 * u + 2))
    for k in range(c):
        pool.indirect_dma_start(g.by_src, bass.IndirectOffsetOnAxis(ap=g.place_st[u][:, k:k + 1], axis=0),
                                g.rec_st[u][:, k, :], None).then_inc(g.sw["scattered"][u], 16)


def build_index(nc, g, layer):
    with ExitStack() as ctx:
        sb, sem, ps = g.maker(ctx)
        loaded, conv, turned, moved = (sem(f"x{layer}_{n}") for n in ("loaded", "conv", "turned", "moved"))
        vals = g.acc[:, 16000:18048].rearrange("p (b w e) -> p b w e", b=4, w=2)
        raw = g.rows[:] if layer == 0 else g.rows[:].rearrange("p b w e -> p b (w e)").rearrange(
            "p b (e w) -> p b w e", w=2)
        pt = [ps(f"pi{layer}{u}", [P, 4, P]) for u in range(4)]
        block = ctx.enter_context(nc.Block())
        if layer == 1:
            @block.sync
            def _(sp):
                sp.dma_start(g.rows[:].rearrange("p b w e -> p (b w e)"),
                             g.by_src.rearrange("(p e) w -> p (e w)", p=P)).then_inc(loaded, 16)

        @block.vector
        def _(dve):
            if layer == 1:
                dve.wait_ge(loaded, 16)
            gat, tgt = (0, 1) if layer == 0 else (1, 0)
            dve.tensor_copy(vals[:, :, 0, :], raw[:, :, gat, :]).then_inc(conv, 1)
            dve.tensor_copy(vals[:, :, 1, :], raw[:, :, tgt, :]).then_inc(conv, 1)
            dve.wait_ge(conv, 2)
            for b in range(4):
                dve.tensor_scalar(vals[:, b, 1, :], vals[:, b, 1, :], g.tile_base[:, layer, b:b + 1], None,
                                  ALU.subtract).then_inc(conv, 1)
            for b in range(4):
                dve.wait_ge(turned, b + 1)
                for w, out in ((0, g.idx), (1, g.key)):
                    dve.tensor_copy(out[:].rearrange("p (k b h) -> p b h k", b=4, h=2)[:, b, :, :],
                                    pt[b][:, 2 * w:2 * w + 2, :]).then_inc(moved, 1)
            dve.wait_ge(moved, 8)

        @block.tensor
        def _(pe):
            pe.wait_ge(conv, 6)
            for b in range(4):
                for w in range(2):
                    for h in range(2):
                        last = pe.transpose(pt[b][:, 2 * w + h, :], vals[:, b, w, h * P:(h + 1) * P], g.ident[:])
                last.then_inc(turned, 1)


def wait_apart(eng, g, sem, value):
    eng.wait_ge(sem, value)
    eng.sem_inc(g.passed, 1)


def layer_norm(dve, st, out, x, stats, mv, norm, n):
    st.mark(dve.bn_stats(stats, x))
    wait_apart(dve, st.g, st.sem, st.value())
    dve.bn_aggr(mv, stats).then_inc(norm[0], 1)
    dve.wait_ge(norm[1], n)
    st.link(dve.reciprocal(mv[:, 1:2], mv[:, 1:2]))
    return dve.tensor_scalar(out, x, mv[:, 0:1], mv[:, 1:2], ALU.subtract, ALU.mult)


def var_root(act, g, mv, norm, n):
    act.wait_ge(norm[0], n)
    act.activation(mv[:, 1:2], mv[:, 1:2], ACT.Sqrt, bias=g.ln_eps[:, 0:1]).then_inc(norm[1], 1)


def project(nc, g):
    with ExitStack() as ctx:
        sb, sem, ps = g.maker(ctx)
        HC = EC // 2
        x_in = [sem(f"a_x{u}") for u in range(2)]
        stored = [sem(f"a_st{u}") for u in range(2)]
        x_free, xn_ready, xT_turned, xT_copied = (sem(f"a_{n}") for n in (
            "x_free", "xn_ready", "turned", "copied"))
        v_ready, v_free, row_ready, step = (sem(f"a_{n}") for n in ("v_ready", "v_free", "row_ready", "step"))
        norm_sems = [sem("a_var"), sem("a_root")]
        emt, emb, e8 = (sem(f"a_{n}") for n in ("emt", "emb", "e8"))
        ranked = sem("a_ranked")
        xs = [sb(f"xs{u}", [P, D]) for u in range(2)]
        xn = [sb(f"xn{u}", [P, D]) for u in range(2)]
        xT = [sb(f"xT{u}", [P, 4, P]) for u in range(2)]
        row = [sb(f"row{u}", [P, W]) for u in range(2)]
        stats, mv = sb("stats", [P, 6]), [sb(f"mv{u}", [P, 2]) for u in range(2)]
        emax = sb("emax", [P, H])
        em8, dg8 = sb("em8", [H, 1]), sb("dg8", [H, H])
        emB = sb("emB", [P, H])
        pos = g.acc[:, 8 * EC:9 * EC]
        run = [g.acc[:, 9 * EC + u * HC:9 * EC + (u + 1) * HC] for u in range(2)]
        mask = [g.acc[:, 11 * EC + u * HC:11 * EC + (u + 1) * HC].bitcast(BF16)[:, 0:HC] for u in range(2)]
        pT = [ps(f"pT{u}", [P, 4, P]) for u in range(2)]
        pV = [ps(f"pV{u}", [P, D]) for u in range(2)]
        pE = [ps(f"pE{u}", [P, 2 * H]) for u in range(2)]
        pM = ps("pM", [P, P])
        block = ctx.enter_context(nc.Block())

        @block.sync
        def _(sp):
            with sp.Fori(0, NT // 2) as i:
                for u in range(2):
                    sp.wait_ge(x_free, 2 * i + (u + 1))
                    sp.dma_start(xs[u][:], g.x[bass.ds((i * 2 + u) * P, P), :]).then_inc(x_in[u], 16)

        @block.gpsimd
        def _(pool):
            pool.wait_ge(ranked, 1)
            for u in range(2):
                scatter_records(pool, g, 0, 0, u)
            with pool.Fori(1, SCAT[0][0]) as i:
                for u in range(2):
                    scatter_records(pool, g, 0, i, u)

        @block.vector
        def _(dve):
            st = Steps(dve, step, g)
            dve.sem_inc(x_free, 2)
            dve.sem_inc(v_free, 2)
            for u in range(2):
                dve.sem_inc(stored[u], 16)
            st.link(dve.memset(emax[:], -3e38))

            def norm(i, u):
                dve.wait_ge(x_in[u], 16 * i + 16)
                if not isinstance(i, int):
                    dve.wait_ge(xT_turned, 2 * i + (u - 1))
                st.link(layer_norm(dve, st, xn[u][:], xs[u][:], stats[:], mv[u][:], norm_sems, 2 * i + (u + 1)))
                dve.sem_inc(x_free, 1)
                dve.sem_inc(xn_ready, 1)

            def finish(i, u):
                n = 2 * i + u
                dve.wait_ge(v_ready, n + 1)
                dve.wait_ge(stored[u], 16 * i + 16)
                st.mark(dve.tensor_tensor(row[u][:, 0:D], pV[u][:], g.bv[:], ALU.add))
                st.mark(dve.tensor_tensor(row[u][:, D:W], pE[u][:, 0:H], g.blr[:, 0:H], ALU.add))
                st.link(dve.tensor_tensor(g.erm[:, bass.ds((2 * i + u) * 2 * H, H)], pE[u][:, H:2 * H],
                                          g.blr[:, H:2 * H], ALU.add))
                dve.sem_inc(v_free, 1)
                dve.sem_inc(row_ready, 1)
                st.link(dve.tensor_tensor(emax[:], emax[:], row[u][:, D:W], ALU.max))

            def rank(half, tiles):
                col = slice(half * HC, (half + 1) * HC)
                two = list(enumerate(tiles))
                for v, b in two:
                    st.mark(dve.tensor_scalar(mask[v], g.src_tile[:, col], g.tiota[:, bass.ds(b, 1)], None, ALU.is_equal))
                for v, b in two:
                    dve.wait_ge(step, st.value() - (len(two) - 1))
                    st.mark(dve.tensor_tensor_scan(run[v], mask[v], g.zeros[:, col], g.bucket_base[:, bass.ds(b, 1)],
                                                   ALU.add, ALU.add))
                for v, b in two:
                    wait_apart(dve, g, step, st.value())
                    if half == 0:
                        st.mark(dve.tensor_copy(g.bucket_base[:, bass.ds(b, 1)], run[v][:, HC - 1:HC]))
                    st.mark(dve.copy_predicated(pos[:, col], mask[v].bitcast(I16), run[v]))
                dve.wait_ge(step, st.value())

            def placed(half):
                col = slice(half * HC, (half + 1) * HC)
                st.link(dve.tensor_copy(g.place[:, col], pos[:, col]))

            def two(i, tiles=()):
                for u in range(2):
                    norm(i + 1, u)
                    if tiles:
                        rank(1, tiles[2 * u:2 * u + 2])
                    finish(i, u)

            with dve.Fori(0, T // 8) as i:
                st.enter(i, 8 * 4)
                for b in range(0, 8, 2):
                    rank(0, (8 * i + b, 8 * i + (b + 1)))
            st.leave(T // 8)
            rank(0, (T - 1,))
            placed(0)
            dve.sem_inc(ranked, 1)
            norm(0, 0)
            norm(0, 1)
            rank(1, (T - 1,))
            with dve.Fori(0, T // 4) as i:
                st.enter(i, 14 + 12)
                two(i, [4 * i + b for b in range(4)])
            st.leave(T // 4)
            placed(1)
            with dve.Fori(T // 4, NT // 2 - 1) as i:
                st.enter(i - T // 4, 14)
                two(i)
            st.leave(NT // 2 - 1 - T // 4)
            finish(NT // 2 - 1, 0)
            finish(NT // 2 - 1, 1)
            dve.sem_inc(emt, 1)
            dve.wait_ge(emt, 2)
            st.link(dve.tensor_reduce(em8[:], pM[0:H, :], AX.X, ALU.max))
            dve.tensor_scalar(dg8[:], g.ident[0:H, 0:H], em8[:, 0:1], None, ALU.mult).then_inc(e8, 1)
            dve.wait_ge(emb, 1)
            st.link(dve.tensor_copy(emB[:], pM[:, 0:H]))
            er = g.erm[:].rearrange("p (t c) -> p t c", c=2 * H)
            m, e = er[:, :, H:2 * H], er[:, :, 0:H]
            st.link(dve.tensor_tensor(m, e, emB[:].unsqueeze(1).to_broadcast([P, NT, H]), ALU.add))
            st.link(dve.scalar_tensor_tensor(out=m, in0=m, scalar=0.2, in1=m, op0=ALU.mult, op1=ALU.max))

        @block.tensor
        def _(pe):
            def turn(i, u):
                pe.wait_ge(xn_ready, 2 * i + (u + 1))
                for c in range(4):
                    last = pe.transpose(pT[u][:, c, :], xn[u][:, c * P:(c + 1) * P], g.ident[:])
                last.then_inc(xT_turned, 1)

            def mult(i, u):
                pe.wait_ge(xT_copied, 2 * i + (u + 1))
                pe.wait_ge(v_free, 2 * i + (u + 1))
                for c in range(4):
                    pe.matmul(pV[u][:], xT[u][:, c, :], g.Wv[:, c, :], start=(c == 0), stop=(c == 3))
                    last = pe.matmul(pE[u][:], xT[u][:, c, :], g.Wlr[:, c, :], start=(c == 0), stop=(c == 3))
                last.then_inc(v_ready, 1)

            def two(i, last):
                turn(i, 1)
                mult(i, 0)
                if not last:
                    turn(i + 1, 0)
                mult(i, 1)

            turn(0, 0)
            with pe.Fori(0, NT // 2 - 1) as i:
                two(i, False)
            two(NT // 2 - 1, True)
            pe.wait_ge(emt, 1)
            pe.transpose(pM[0:H, :], emax[:], g.ident[:]).then_inc(emt, 1)
            pe.wait_ge(e8, 1)
            pe.matmul(pM[:, 0:H], g.ones[0:H, :], dg8[:], start=True, stop=True).then_inc(emb, 1)

        @block.scalar
        def _(act):
            def copy(i, u):
                act.wait_ge(xT_turned, 2 * i + (u + 1))
                act.activation(xT[u][:], pT[u][:], ACT.Copy).then_inc(xT_copied, 1)

            def root(i, u):
                var_root(act, g, mv[u], norm_sems, 2 * i + (u + 1))

            def store(i, u):
                act.wait_ge(row_ready, 2 * i + (u + 1))
                act.dma_start(g.ve[bass.ds((i * 2 + u) * P, P), :], row[u][:]).then_inc(stored[u], 16)

            root(0, 0)
            root(0, 1)
            copy(0, 0)
            with act.Fori(0, NT // 2 - 1) as i:
                copy(i, 1)
                root(i + 1, 0)
                store(i, 0)
                copy(i + 1, 0)
                root(i + 1, 1)
                store(i, 1)
            copy(NT // 2 - 1, 1)
            store(NT // 2 - 1, 0)
            store(NT // 2 - 1, 1)
            for u in range(2):
                act.wait_ge(stored[u], 16 * (NT // 2) + 16)


def edge_pass(nc, g, layer):
    attend = layer == 0
    width = W if attend else D
    table = g.ve if attend else g.z
    AHEAD = 3 if attend else 2
    ADDS = 2 if attend else 1
    CH = 4 * QI
    with ExitStack() as ctx:
        sb, sem, ps = g.maker(ctx)
        n_ = f"e{layer}_"
        got = g.sw[f"got{layer}"]
        staged, zeroed = sem(n_ + "staged"), sem(n_ + "zeroed")
        hot, hot_turned, hot_copied, scored, logit, weight, scaled = (sem(n_ + x) for x in (
            "hot", "turned", "copied", "scored", "logit", "weight", "scaled"))
        summed, chain, acc_step = (sem(n_ + x) for x in ("summed", "chain", "acc"))
        G = sb(f"G{layer}", [P, CH, width])
        idx_st = sb(f"idx_st{layer}", [P, CH], I32)
        S = [sb(f"S{layer}{u}", [P, 4, P]) for u in range(QI)]
        NA = 2 if attend else 4
        pA = [ps(f"pA{layer}{u}", [P, D]) for u in range(NA)]
        if attend:
            ST = [sb(f"ST{u}", [P, 4, P]) for u in range(2)]
            sc = [sb(f"sc{u}", [P, 4, H]) for u in range(2)]
            pS = [ps(f"pS{u}", [P, 4, P]) for u in range(2)]
            pE = [ps(f"pEd{u}", [P, 4, 2 * H]) for u in range(2)]
            pD = [ps(f"pD{u}", [P, H]) for u in range(NA)]
        block = ctx.enter_context(nc.Block())

        def tiles_of(engine, i, q):
            ids = g.tiles[0:1, bass.ds(i * (2 * QI) + (layer * WL + 2 * q), 2)]
            return nc.values_load_multi_w_load_instructions(ids, engines=[engine], min_val=0, max_val=T - 1)[1]

        def laps(eng, body):
            body(0, True, False)
            with eng.Fori(1, ITER - 1) as i:
                body(i, False, False)
            body(ITER - 1, False, True)

        @block.gpsimd
        def _(pool):
            def stage(i, h, first):
                if not first:
                    for u in range(h * 8, h * 8 + 8):
                        pool.wait_ge(got[u], 16 * i)
                pool.tensor_copy(idx_st[:, h * 8:h * 8 + 8], g.idx[:, bass.ds(i * CH + h * 8, 8)]).then_inc(staged, 1)

            def lap(i, first, last):
                for h in range(2):
                    wait_apart(pool, g, staged, 2 * i + (h + 1))
                    for u in range(h * 8, h * 8 + 8):
                        if not first and u % 4 == 0:
                            wait_apart(pool, g, summed, (i - 1) * (2 * QI) + (u // 2 + 2))
                        pool.indirect_dma_start(G[:, u, :], None, table,
                                                bass.IndirectOffsetOnAxis(ap=idx_st[:, u:u + 1], axis=0))\
                            .then_inc(got[u], 16)
                        if u == h * 8 + 6:
                            if h == 0:
                                stage(i, 1, first)
                            elif not last:
                                stage(i + 1, 0, False)
                    if attend:
                        scatter_records(pool, g, 1, i, h)

            stage(0, 0, True)
            laps(pool, lap)

        @block.vector
        def _(dve):
            dve.memset(g.acc[:], 0.0).then_inc(zeroed, 1)
            dve.wait_ge(zeroed, 1)

            def one_hot(i, q):
                if not (isinstance(i, int) and i == 0):
                    dve.wait_ge(summed, (i - 1) * (2 * QI) + (2 * q + 2))
                k = g.key[:, bass.ds(i * CH + 4 * q, 4)].unsqueeze(2).to_broadcast([P, 4, P])
                dve.tensor_tensor(S[q][:], g.iota[:].unsqueeze(1).to_broadcast([P, 4, P]), k, ALU.is_equal)\
                   .then_inc(hot, 1)

            def score(i, q, part):
                Q = i * QI + q
                t, e = sc[q % 2][:], pE[q % 2][:]
                if part == 0:
                    for u in range(4 * q, 4 * q + 4):
                        dve.wait_ge(got[u], 16 * i + 16)
                    dve.wait_ge(scored, Q + 1)
                    dve.tensor_tensor(t, G[:, 4 * q:4 * q + 4, D:W], e[:, :, 0:H], ALU.add).then_inc(chain, 1)
                elif part == 1:
                    dve.wait_ge(chain, 2 * Q + 1)
                    dve.scalar_tensor_tensor(out=t, in0=t, scalar=0.2, in1=t, op0=ALU.mult, op1=ALU.max)\
                       .then_inc(chain, 1)
                else:
                    dve.wait_ge(chain, 2 * Q + 2)
                    dve.tensor_tensor(t, t, e[:, :, H:2 * H], ALU.subtract).then_inc(logit, 1)

            def scale(i, q, u):
                dve.wait_ge(weight, i * QI + (q + 1))
                v = G[:, 4 * q + u, 0:D].rearrange("p (h f) -> p h f", h=H)
                dve.tensor_tensor(v, v, G[:, 4 * q + u, D:W].unsqueeze(2).to_broadcast([P, H, F]), ALU.mult)\
                   .then_inc(scaled, 1)

            def add(i, q, p, t):
                k = i * (2 * QI) + (2 * q + p)
                b = (2 * q + p) % NA
                dve.wait_ge(summed, k + 1)
                if not (isinstance(k, int) and k == 0):
                    dve.wait_ge(acc_step, k * ADDS)
                a = g.acc[:, bass.ds(t * W, D)]
                dve.tensor_tensor(a, a, pA[b][:], ALU.add).then_inc(acc_step, 1)
                if attend:
                    a = g.acc[:, bass.ds(t * W + D, H)]
                    dve.tensor_tensor(a, a, pD[b][:], ALU.add).then_inc(acc_step, 1)

            def lap(i, first, last):
                for q in range(QI):
                    prev = (i, q - 1) if q else (i - 1, QI - 1)
                    adds = not (first and q == 0)
                    if adds:
                        tiles = tiles_of(mybir.EngineType.DVE, *prev)
                        add(*prev, 0, tiles[0])
                    if not (last and q >= QI - AHEAD):
                        one_hot(i + (q + AHEAD) // QI, (q + AHEAD) % QI)
                    if adds:
                        add(*prev, 1, tiles[1])
                    if attend:
                        weighs, scores = not (last and q >= QI - 1), not (last and q >= QI - 2)
                        for u in range(4):
                            if scores and u < 3:
                                score(i + (q + 2) // QI, (q + 2) % QI, u)
                            if weighs:
                                scale(i + (q + 1) // QI, (q + 1) % QI, u)

            for q in range(AHEAD):
                one_hot(0, q)
            if attend:
                for q in range(2):
                    for part in range(3):
                        score(0, q, part)
                for u in range(4):
                    scale(0, 0, u)
            laps(dve, lap)
            tiles = tiles_of(mybir.EngineType.DVE, ITER - 1, QI - 1)
            for p in range(2):
                add(ITER - 1, QI - 1, p, tiles[p])

        @block.tensor
        def _(pe):
            def turn(i, q):
                Q = i * QI + q
                pe.wait_ge(hot, Q + 1)
                for u in range(4):
                    last = pe.transpose(pS[q % 2][:, u, :], S[q][:, u, :], g.ident[:])
                last.then_inc(hot_turned, 1)

            def spread(i, q):
                tiles = tiles_of(mybir.EngineType.PE, i, q)
                pe.wait_ge(hot_copied, i * QI + (q + 1))
                for p in range(2):
                    t = tiles[p]
                    for u in (2 * p, 2 * p + 1):
                        last = pe.matmul(pE[q % 2][:, u, :], ST[q % 2][:, u, :], g.erm[:, bass.ds(t * 2 * H, 2 * H)],
                                         start=True, stop=True)
                last.then_inc(scored, 1)

            def reduce(i, q, p):
                k = 2 * q + p
                if not (isinstance(i, int) and i == 0 and k < NA):
                    pe.wait_ge(acc_step, (i * (2 * QI) + (k - NA + 1)) * ADDS)
                if attend:
                    pe.wait_ge(scaled, i * CH + (2 * k + 2))
                else:
                    pe.wait_ge(hot, i * QI + (q + 1))
                    for u in (0, 1):
                        pe.wait_ge(got[2 * k + u], 16 * i + 16)
                for u in (0, 1):
                    s = S[q][:, 2 * p + u, :]
                    last = pe.matmul(pA[k % NA][:], s, G[:, 2 * k + u, 0:D], start=(u == 0), stop=(u == 1))
                    if attend:
                        last = pe.matmul(pD[k % NA][:], s, G[:, 2 * k + u, D:W], start=(u == 0), stop=(u == 1))
                last.then_inc(summed, 1)

            def lap(i, first, last):
                for q in range(QI):
                    if attend and not (last and q >= QI - 2):
                        spread(i + (q + 2) // QI, (q + 2) % QI)
                    reduce(i, q, 0)
                    if attend and not (last and q >= QI - 3):
                        turn(i + (q + 3) // QI, (q + 3) % QI)
                    reduce(i, q, 1)

            if attend:
                turn(0, 0)
                turn(0, 1)
                spread(0, 0)
                turn(0, 2)
                spread(0, 1)
            laps(pe, lap)

        if attend:
            @block.scalar
            def _(act):
                def copy(i, q):
                    act.wait_ge(hot_turned, i * QI + (q + 1))
                    if not (isinstance(i, int) and i == 0 and q < 2):
                        act.wait_ge(scored, i * QI + (q - 1))
                    act.activation(ST[q % 2][:], pS[q % 2][:], ACT.Copy).then_inc(hot_copied, 1)

                def weigh(i, q):
                    act.wait_ge(logit, i * QI + (q + 1))
                    act.activation(G[:, 4 * q:4 * q + 4, D:W], sc[q % 2][:], ACT.Exp).then_inc(weight, 1)

                def lap(i, first, last):
                    for q in range(QI):
                        if not (last and q >= QI - 3):
                            copy(i + (q + 3) // QI, (q + 3) % QI)
                        if not (last and q >= QI - 2):
                            weigh(i + (q + 2) // QI, (q + 2) % QI)

                copy(0, 0)
                copy(0, 1)
                weigh(0, 0)
                copy(0, 2)
                weigh(0, 1)
                laps(act, lap)


def wavelet_ffn(nc, g):
    M = NT // 2
    with ExitStack() as ctx:
        sb, sem, ps = g.maker(ctx)
        x_in, stored = ([sem(f"b_{n}{u}") for u in range(2)] for n in ("x", "st"))
        x_free, step, yc_ready, vars_ready, rooted = (sem(f"b_{n}") for n in (
            "x_free", "step", "yc_ready", "vars", "rooted"))
        low, low_copied, hid, hid_done, delta_ready, row_ready = (sem(f"b_{n}") for n in (
            "low", "low_copied", "hid", "hid_done", "delta", "row_ready"))
        xs, x1, y, x2, z = ([sb(f"w{n}{u}", [P, D]) for u in range(2)] for n in ("xs", "x1", "y", "x2", "z"))
        s, yc = ([[sb(f"w{n}{k}{u}", [P, w]) for u in range(2)] for k in range(2)] for n, w in (("s", D), ("yc", HID)))
        lT, hT = sb("lT", [P, 2, P]), sb("hT", [P, 2, 2 * P])
        rd, stats, mv = sb("rd", [P, NT, H]), sb("wstats", [P, 4, 6]), sb("wmv", [P, 4, 2])
        pL, pH = ps("pL", [P, 2, P]), ps("pH", [P, 2, P])
        pX = [[ps(f"pX{k}{u}", [P, HID]) for u in range(2)] for k in range(2)]
        block = ctx.enter_context(nc.Block())

        @block.sync
        def _(sp):
            with sp.Fori(0, M) as i:
                for u in range(2):
                    sp.wait_ge(x_free, 2 * i + (u + 1))
                    sp.dma_start(xs[u][:], g.x[bass.ds((i * 2 + u) * P, P), :]).then_inc(x_in[u], 16)

        @block.gpsimd
        def _(pool):
            for u in range(2):
                scatter_records(pool, g, 2, 0, u)
            with pool.Fori(1, SCAT[2][0]) as i:
                for u in range(2):
                    scatter_records(pool, g, 2, i, u)
            for u in range(2):
                pool.wait_ge(g.sw["scattered"][u], 16 * (EC // 2))

        @block.vector
        def _(dve):
            st = Steps(dve, step, g)
            dve.sem_inc(x_free, 2)
            for u in range(2):
                dve.sem_inc(stored[u], 32)
            den = g.acc.rearrange("p (t w) -> p t w", w=W)[:, :, D:W]
            st.link(dve.tensor_scalar(rd[:], den, 1e-30, None, ALU.max))
            st.link(dve.reciprocal(rd[:], rd[:]))
            rd_flat = rd[:].rearrange("p t h -> p (t h)")

            def lap(i, par, n, front, back):
                m = i + 2
                norms = [u for u in range(2) if front] + [2 + u for u in range(2) if back]
                at = {}
                if front:
                    for u in range(2):
                        a = g.acc[:, bass.ds(m * (2 * W) + u * W, D)].rearrange("p (h f) -> p h f", h=H)
                        r = rd_flat[:, bass.ds(m * (2 * H) + u * H, H)].unsqueeze(2).to_broadcast([P, H, F])
                        st.mark(dve.tensor_tensor(x1[u][:].rearrange("p (h f) -> p h f", h=H), a, r, ALU.mult))
                        at[u] = st.value()
                if back:
                    for u in range(2):
                        dve.wait_ge(delta_ready, 2 * i + (u + 1))
                        dve.wait_ge(stored[u], 32 * i + 32)
                        st.mark(dve.scalar_tensor_tensor(
                            out=x2[u][:].rearrange("p (j c) -> p j c", c=2),
                            in0=pX[par][u][:].unsqueeze(2).to_broadcast([P, HID, 2]), scalar=0.5,
                            in1=s[par][u][:].rearrange("p (j c) -> p j c", c=2), op0=ALU.mult, op1=ALU.add))
                        at[2 + u] = st.value()
                if front:
                    for u in range(2):
                        dve.wait_ge(x_in[u], m * 16 + 16)
                        dve.wait_ge(step, at[u])
                        st.mark(dve.tensor_tensor(x1[u][:], x1[u][:], xs[u][:], ALU.add))
                        at[u] = st.value()
                for k in reversed(norms):
                    dve.wait_ge(step, at[k])
                    if k < 2:
                        dve.sem_inc(x_free, 1)
                    st.mark(dve.bn_stats(stats[:, k, :], (x1[k] if k < 2 else x2[k - 2])[:]))
                wait_apart(dve, g, step, st.value())
                for k in norms:
                    dve.bn_aggr(mv[:, k, :], stats[:, k, :]).then_inc(vars_ready, 1)
                dve.wait_ge(rooted, n)
                var = mv[:, norms[0]:norms[-1] + 1, 1]
                st.link(dve.reciprocal(var, var))
                for k in norms:
                    x, out = (x1[k], y[k]) if k < 2 else (x2[k - 2], z[k - 2])
                    st.mark(dve.tensor_scalar(out[:], x[:], mv[:, k, 0:1], mv[:, k, 1:2], ALU.subtract, ALU.mult))
                dve.wait_ge(step, st.value())
                if back:
                    dve.sem_inc(row_ready, 1)
                if front:
                    for u in range(2):
                        v = y[u][:].rearrange("p (j c) -> p j c", c=2)
                        st.mark(dve.tensor_tensor(yc[par][u][:], v[:, :, 0], v[:, :, 1], ALU.add))
                    dve.wait_ge(step, st.value())
                    dve.sem_inc(yc_ready, 1)
                    for u in range(2):
                        st.mark(dve.tensor_tensor(s[par][u][:], x1[u][:], y[u][:], ALU.add))
                    dve.wait_ge(step, st.value())

            lap(-2, 0, 1, True, False)
            lap(-1, 1, 2, True, False)
            with dve.Fori(0, (M - 3) // 2) as j:
                st.enter(j, 2 * 19)
                for par in range(2):
                    lap(2 * j + par, par, 2 * j + (par + 3), True, True)
            st.leave((M - 3) // 2)
            lap(M - 3, 0, M, True, True)
            lap(M - 2, 1, M + 1, False, True)
            lap(M - 1, 0, M + 2, False, True)

        @block.tensor
        def _(pe):
            def one(m, par):
                c_ = yc[par]
                pe.wait_ge(yc_ready, m + 1)
                for u in range(2):
                    for c in range(2):
                        last = pe.matmul(pL[:, c, u * 64:(u + 1) * 64], c_[u][:, c * P:(c + 1) * P], g.pairup[:],
                                         start=True, stop=True)
                last.then_inc(low, 1)
                pe.wait_ge(low_copied, m + 1)
                for o in range(2):
                    for c in range(2):
                        last = pe.matmul(pH[:, o, :], g.Wf[:, c, o * P:(o + 1) * P], lT[:, c, :],
                                         start=(c == 0), stop=(c == 1))
                last.then_inc(hid, 1)
                for u in range(2):
                    pe.matmul(pX[par][u][:], g.unpair[:], c_[u][:], start=True, stop=False)
                    pe.matmul(pX[par][u][:], g.ones[0:1, :], g.fc2b[:], start=False, stop=False)
                pe.wait_ge(hid_done, m + 1)
                for u in range(2):
                    for o in range(2):
                        last = pe.matmul(pX[par][u][:], hT[:, o, u * P:(u + 1) * P], g.fc2T[:, o, :], start=False, stop=(o == 1))
                    last.then_inc(delta_ready, 1)

            with pe.Fori(0, M // 2) as j:
                for par in range(2):
                    one(2 * j + par, par)
            one(M - 1, 0)

        @block.scalar
        def _(act):
            def root(n, k0, k1, v):
                act.wait_ge(vars_ready, v)
                act.activation(mv[:, k0:k1, 1], mv[:, k0:k1, 1], ACT.Sqrt, bias=g.ln_eps[:, 0:1]).then_inc(rooted, 1)

            def mid(m):
                act.wait_ge(low, m + 1)
                act.activation(lT[:], pL, ACT.Copy).then_inc(low_copied, 1)
                act.wait_ge(hid, m + 1)
                for o in range(2):
                    last = act.activation(hT[:, o, :].rearrange("p (i c) -> p i c", c=2),
                                          pH[:, o, :].unsqueeze(2).to_broadcast([P, P, 2]),
                                          ACT.Gelu, bias=g.fc1b[:, o:o + 1])
                last.then_inc(hid_done, 1)

            def store(i):
                act.wait_ge(row_ready, i + 1)
                for u in range(2):
                    rows = bass.ds(i * (2 * P) + u * P, P)
                    act.dma_start(g.x2[rows, :], x2[u][:]).then_inc(stored[u], 16)
                    act.dma_start(g.z[rows, :], z[u][:]).then_inc(stored[u], 16)

            root(1, 0, 2, 2)
            mid(0)
            root(2, 0, 2, 4)
            with act.Fori(0, M - 2) as i:
                mid(i + 1)
                root(i + 3, 0, 4, 4 * i + 8)
                store(i)
            done = 4 + 4 * (M - 2)
            mid(M - 1)
            root(M + 1, 2, 4, done + 2)
            store(M - 2)
            root(M + 2, 2, 4, done + 4)
            store(M - 1)
            for u in range(2):
                act.wait_ge(stored[u], 32 * M + 32)


def gin_mlp(nc, g):
    M = NT // 2
    with ExitStack() as ctx:
        sb, sem, ps = g.maker(ctx)
        loaded = sem("m_loaded")
        z_in, x2_in, stored = ([sem(f"m_{n}{u}") for u in range(2)] for n in ("z", "x2", "st"))
        z_free, x2_free, step, h0_ready, h0_turned, h0_copied = (sem(f"m_{n}") for n in (
            "z_free", "x2_free", "step", "h0", "h0t", "h0c"))
        h1_ready, h1_done, o_ready, xb_ready, q_ready, q_turned, q_copied, lg_ready = (
            sem(f"m_{n}") for n in ("h1", "h1d", "o", "xb", "q", "qt", "qc", "lg"))
        norm1, norm2 = [sem("m_var1"), sem("m_root1")], [sem("m_var2"), sem("m_root2")]
        W1, W2 = sb("gW1", [P, 4, D]), sb("gW2", [P, 4, D])
        b1, b2, gam, bet = sb("gb1", [P, 4]), sb("gb2", [P, D]), sb("gam", [P, D]), sb("bet", [P, D])
        Wr = sb("gWr", [P, 4, NX])
        zs, x2, xb, x3, q = ([sb(f"m{n}{u}", [P, D]) for u in range(2)] for n in ("zs", "x2", "xb", "x3", "q"))
        h0 = [sb(f"h0{u}", [P, D]) for u in range(2)]
        o = sb("o", [P, D])
        h0T = [sb(f"h0T{u}", [P, 4, P]) for u in range(2)]
        h1T = [sb(f"h1T{u}", [P, 4, P]) for u in range(2)]
        qT = sb("qT", [P, 4, P])
        stats, mv1, mv2 = sb("mstats", [P, 6]), sb("mmv1", [P, 2]), sb("mmv2", [P, 2])
        pT, pQ, pG = ps("mpT", [P, 4, P]), ps("mpQ", [P, 4, P]), ps("mpG", [P, NT, NX])
        pH = [ps(f"mpH{u}", [P, 4, P]) for u in range(2)]
        pO = [ps(f"mpO{u}", [P, D]) for u in range(2)]
        g_flat = pG.rearrange("p t e -> p (t e)")
        block = ctx.enter_context(nc.Block())

        @block.sync
        def _(sp):
            for w, d in ((W1, g.gW1T), (W2, g.gW2T), (Wr, g.Wr)):
                sp.dma_start(w[:], d.rearrange("(c p) n -> p c n", p=P)).then_inc(loaded, 16)
            sp.dma_start(b1[:], g.gb1).then_inc(loaded, 16)
            for w, d in ((b2, g.gb2), (gam, g.gamma), (bet, g.beta)):
                sp.dma_start(w[:], d.to_broadcast([P, D])).then_inc(loaded, 16)
            with sp.Fori(0, NT // 2) as i:
                for u in range(2):
                    rows = bass.ds((i * 2 + u) * P, P)
                    sp.wait_ge(z_free, 2 * i + (u + 1))
                    sp.dma_start(zs[u][:], g.z[rows, :]).then_inc(z_in[u], 16)
                    sp.wait_ge(x2_free, 2 * i + (u + 1))
                    sp.dma_start(x2[u][:], g.x2[rows, :]).then_inc(x2_in[u], 16)

        @block.gpsimd
        def _(pool):
            pool.sem_inc(x2_free, 2)
            pool.wait_ge(loaded, 16 * 7)

            def one(i, u):
                pool.wait_ge(x2_in[u], 16 * i + 16)
                if not isinstance(i, int):
                    pool.wait_ge(q_ready, 2 * i + (u - 1))
                pool.tensor_tensor(xb[u][:], x2[u][:], bet[:], ALU.add).then_inc(xb_ready, 1)
                pool.wait_ge(xb_ready, 2 * i + (u + 1))
                pool.sem_inc(x2_free, 1)

            one(0, 0)
            one(0, 1)
            with pool.Fori(1, NT // 2) as i:
                one(i, 0)
                one(i, 1)

        @block.vector
        def _(dve):
            st = Steps(dve, step, g)
            dve.sem_inc(z_free, 2)
            for u in range(2):
                dve.sem_inc(stored[u], 32)
            dve.wait_ge(loaded, 16 * 7)

            def front(i, u):
                dve.wait_ge(z_in[u], 16 * i + 16)
                if not isinstance(i, int):
                    dve.wait_ge(h0_turned, 2 * i + (u - 1))
                st.link(dve.scalar_tensor_tensor(out=h0[u][:], in0=zs[u][:], scalar=g.epsb[:, 0:1],
                                                 in1=g.acc[:, bass.ds((2 * i + u) * W, D)], op0=ALU.mult, op1=ALU.add))
                dve.sem_inc(h0_ready, 1)
                dve.sem_inc(z_free, 1)

            def back(i, u):
                n = 2 * i + u
                dve.wait_ge(o_ready, n + 1)
                st.link(dve.tensor_tensor(o[:], pO[u][:], b2[:], ALU.add))
                st.link(layer_norm(dve, st, o[:], o[:], stats[:], mv1[:], norm1, n + 1))
                st.link(dve.tensor_tensor(o[:], o[:], gam[:], ALU.mult))
                dve.wait_ge(xb_ready, n + 1)
                dve.wait_ge(stored[u], 32 * i + 32)
                st.link(dve.tensor_tensor(x3[u][:], o[:], xb[u][:], ALU.add))
                st.link(layer_norm(dve, st, q[u][:], x3[u][:], stats[:], mv2[:], norm2, n + 1))
                dve.sem_inc(q_ready, 1)

            front(0, 0)
            front(0, 1)
            with dve.Fori(0, M - 1) as i:
                st.enter(i, 20)
                for u in range(2):
                    front(i + 1, u)
                    back(i, u)
            st.leave(M - 1)
            back(M - 1, 0)
            back(M - 1, 1)
            dve.wait_ge(lg_ready, NT)
            st.link(dve.tensor_copy(g.lg[:].rearrange("p e t -> p t e"), pG))

        @block.tensor
        def _(pe):
            pe.wait_ge(loaded, 16 * 7)

            def turn(i, u):
                pe.wait_ge(h0_ready, 2 * i + (u + 1))
                for c in range(4):
                    last = pe.transpose(pT[:, c, :], h0[u][:, c * P:(c + 1) * P], g.ident[:])
                last.then_inc(h0_turned, 1)

            def layer1(i, u):
                pe.wait_ge(h0_copied, 2 * i + (u + 1))
                for o_ in range(4):
                    for c in range(4):
                        last = pe.matmul(pH[u][:, o_, :], W1[:, c, o_ * P:(o_ + 1) * P], h0T[u][:, c, :],
                                         start=(c == 0), stop=(c == 3))
                last.then_inc(h1_ready, 1)

            def layer2(i, u):
                pe.wait_ge(h1_done, 2 * i + (u + 1))
                for c in range(4):
                    last = pe.matmul(pO[u][:], h1T[u][:, c, :], W2[:, c, :], start=(c == 0), stop=(c == 3))
                last.then_inc(o_ready, 1)

            def turn_q(i, u):
                pe.wait_ge(q_ready, 2 * i + (u + 1))
                for c in range(4):
                    last = pe.transpose(pQ[:, c, :], q[u][:, c * P:(c + 1) * P], g.ident[:])
                last.then_inc(q_turned, 1)

            def route(i, u):
                pe.wait_ge(q_copied, 2 * i + (u + 1))
                for c in range(4):
                    last = pe.matmul(g_flat[:, bass.ds((2 * i + u) * NX, NX)], qT[:, c, :], Wr[:, c, :],
                                     start=(c == 0), stop=(c == 3))
                last.then_inc(lg_ready, 1)

            def lap(i, first, last):
                for u in range(2):
                    before = (i, 0) if u else (i - 1, 1)
                    routes = not (first and u == 0)
                    layer2(i, u)
                    if not last:
                        turn(i + 1, u)
                    if routes:
                        turn_q(*before)
                    if not last:
                        layer1(i + 1, u)
                    if routes:
                        route(*before)

            for u in range(2):
                turn(0, u)
                layer1(0, u)
            lap(0, True, False)
            with pe.Fori(1, M - 1) as i:
                lap(i, False, False)
            lap(M - 1, False, True)
            turn_q(M - 1, 1)
            route(M - 1, 1)

        @block.scalar
        def _(act):
            def copy0(i, u):
                act.wait_ge(h0_turned, 2 * i + (u + 1))
                act.activation(h0T[u][:], pT[:], ACT.Copy).then_inc(h0_copied, 1)

            def relu(i, u):
                act.wait_ge(h1_ready, 2 * i + (u + 1))
                for o_ in range(4):
                    last = act.activation(h1T[u][:, o_, :], pH[u][:, o_, :], ACT.Relu, bias=b1[:, o_:o_ + 1])
                last.then_inc(h1_done, 1)

            def copy_q(i, u):
                act.wait_ge(q_turned, 2 * i + (u + 1))
                act.activation(qT[:], pQ[:], ACT.Copy).then_inc(q_copied, 1)

            def store(i, u):
                act.wait_ge(q_ready, 2 * i + (u + 1))
                rows = bass.ds((i * 2 + u) * P, P)
                act.dma_start(g.out[rows, :], x3[u][:]).then_inc(stored[u], 16)
                act.dma_start(g.q[rows, :], q[u][:]).then_inc(stored[u], 16)

            def lap(i, first, last):
                for u in range(2):
                    if not last:
                        copy0(i + 1, u)
                    if not (first and u == 0):
                        copy_q(*((i, 0) if u else (i - 1, 1)))
                    var_root(act, g, mv1, norm1, 2 * i + (u + 1))
                    var_root(act, g, mv2, norm2, 2 * i + (u + 1))
                    if not last:
                        relu(i + 1, u)
                    store(i, u)

            act.wait_ge(loaded, 16 * 7)
            for u in range(2):
                copy0(0, u)
                relu(0, u)
            lap(0, True, False)
            with act.Fori(1, M - 1) as i:
                lap(i, False, False)
            lap(M - 1, False, True)
            copy_q(M - 1, 1)
            for u in range(2):
                act.wait_ge(stored[u], 32 * M + 32)


def choose_tokens(nc, g):
    TB = 10
    NB = NT // TB
    BIS, BU = 32, 8
    NC = CAP // P
    with ExitStack() as ctx:
        sb, sem, ps = g.maker(ctx)
        step, low_read, masked, lohi, turned, diag, spread, exped, summed = (sem(f"r_{n}") for n in (
            "step", "low_read", "masked", "lohi", "turned", "diag", "spread", "exped", "summed"))
        esum, counted, totalled, picked, prefixed, hot, packed, tok_ready, listed = (sem(f"r_{n}") for n in (
            "esum", "counted", "totalled", "picked", "prefixed", "hot", "packed", "tok", "listed"))
        cols = [P, NX, NT]
        L, L2 = g.lg, sb("L2", cols)
        prob, gt, ge, pa, pb_, tot = (sb(f"r{n}", cols) for n in ("prob", "gt", "ge", "pa", "pb", "tot"))
        cmp, lo_d, hi_d, match = (sb(f"r{n}", cols, BF16) for n in ("cmp", "lod", "hid", "match"))
        part = sb("part", [P, NX, NT, 5], BF16)
        R = sb("Rlist", [P, NX, NT, NC, 5], BF16)
        iota_b, ones_b, cnt_b = sb("iota_b", [P, P], BF16), sb("ones_b", [P, P], BF16), sb("cnt_b", [P, NX], BF16)
        zz = sb("rzz", [P, NX * NT])
        digits = sb("digits", [P, 2, NX, NT], I32)
        mm, mr, dg = sb("mm", [P, 2 * NX]), sb("mr", [2 * NX, 1]), sb("dg", [2 * NX, 2 * NX])
        total, cnt = sb("rtotal", [P, NX]), sb("rcnt", [P, NX])
        lo, hi, both, mid = (sb(f"r{n}", [P, NX]) for n in ("lo", "hi", "both", "mid"))
        more, less = sb("more", [P, NX], I32), sb("less", [P, NX], I32)
        start = sb("rstart", [P, 2, NX])
        tok = sb("tok", [P, 2, NT])
        hotb = [sb(f"hotb{u}", [P, TB, P], BF16) for u in range(2)]
        pM, pB, pC = ps("rpM", [2 * NX, P]), ps("rpB", [P, 2 * NX]), ps("rpC", [P, NX])
        pre = [ps(f"rpre{u}", cols) for u in range(2)]
        all_ = [ps(f"rall{u}", cols) for u in range(2)]
        lists_f = [sb(f"lists{u}", [P, NC, 5]) for u in range(2)]
        pK = [p.rearrange("p e t -> p (e t)")[:, 0:5 * NC] for p in pre]
        block = ctx.enter_context(nc.Block())

        R_flat = R[:].rearrange("p e t c v -> p (e t c v)")

        @block.gpsimd
        def _(pool):
            pool.iota(tok[:, 0, :], pattern=[[1, NT]], base=0, channel_multiplier=0,
                      allow_small_or_imprecise_dtypes=True).then_inc(tok_ready, 1)
            pool.iota(tok[:, 1, :], pattern=[[0, NT]], base=0, channel_multiplier=1,
                      allow_small_or_imprecise_dtypes=True).then_inc(tok_ready, 1)
            pool.wait_ge(low_read, 1)
            pool.affine_select(out=L[:], in_=L[:], compare_op=ALU.is_ge, fill=-1e30, base=N - 1,
                               pattern=[[0, NX], [-P, NT]], channel_multiplier=-1).then_inc(masked, 1)

        @block.scalar
        def _(act):
            act.wait_ge(summed, 1)
            act.activation(prob[:], prob[:], ACT.Exp).then_inc(exped, 1)

        @block.tensor
        def _(pe):
            pe.wait_ge(lohi, 1)
            pe.transpose(pM[:], mm[:], g.ident[:]).then_inc(turned, 1)
            pe.wait_ge(diag, 1)
            pe.matmul(pB[:], g.ones[0:2 * NX, :], dg[:], start=True, stop=True).then_inc(spread, 1)
            pe.wait_ge(esum, 1)
            pe.matmul(pB[:, 0:NX], g.ones[:], total[:], start=True, stop=True).then_inc(spread, 1)
            with pe.Fori(0, BIS // BU) as i:
                for j in range(BU):
                    pe.wait_ge(counted, i * BU + (j + 1))
                    pe.matmul(pC[:], ones_b[:], cnt_b[:], start=True, stop=True).then_inc(totalled, 1)
            pe.wait_ge(picked, 1)
            for u, m in enumerate((gt, ge)):
                v = m[:].rearrange("p e t -> p (e t)")
                pe.matmul(pre[u].rearrange("p e t -> p (e t)"), g.upper[:], v, start=True, stop=True)
                pe.matmul(all_[u].rearrange("p e t -> p (e t)"), g.ones[:], v, start=True, stop=True)\
                  .then_inc(prefixed, 1)

            def pack(i, first_lap):
                for j in range(2 * NB):
                    x, b = j // NB, j % NB
                    if b == 0 and not first_lap:
                        pe.wait_ge(listed, 2 * i + (x - 1))
                    pe.wait_ge(hot, i * (2 * NB) + (j + 1))
                    for t in range(TB):
                        first, end = (b == 0 and t == 0), (b == NB - 1 and t == TB - 1)
                        r = R_flat[:, bass.ds(i * (2 * NT * 5 * NC) + (x * NT + b * TB + t) * (5 * NC), 5 * NC)]
                        last = pe.matmul(pK[x], hotb[j % 2][:, t, :], r, start=first, stop=end)
                    last.then_inc(packed, 1)

            pack(0, True)
            with pe.Fori(1, NX // 2) as i:
                pack(i, False)

        @block.vector
        def _(dve):
            st = Steps(dve, step, g)
            st.mark(dve.memset(zz[:], 0.0))
            st.mark(dve.tensor_copy(iota_b[:], g.iota[:]))
            st.mark(dve.tensor_copy(ones_b[:], g.ones[:]))
            st.link(dve.tensor_reduce(mm[:, NX:2 * NX], L[:], AX.X, ALU.min))
            dve.sem_inc(low_read, 1)
            st.link(dve.tensor_scalar(mm[:, NX:2 * NX], mm[:, NX:2 * NX], -1.0, 1.0, ALU.mult, ALU.add))
            dve.wait_ge(masked, 1)
            st.mark(dve.tensor_scalar(L2[:], L[:], 2.0, None, ALU.mult))
            st.link(dve.tensor_reduce(mm[:, 0:NX], L[:], AX.X, ALU.max))
            dve.sem_inc(lohi, 1)
            dve.wait_ge(turned, 1)
            st.link(dve.tensor_reduce(mr[:], pM[:], AX.X, ALU.max))
            st.link(dve.tensor_scalar(dg[:], g.ident[0:2 * NX, 0:2 * NX], mr[:, 0:1], None, ALU.mult))
            dve.sem_inc(diag, 1)
            dve.wait_ge(spread, 1)
            st.mark(dve.tensor_copy(hi[:], pB[:, 0:NX]))
            st.link(dve.tensor_scalar(lo[:], pB[:, NX:2 * NX], -1.0, None, ALU.mult))
            st.link(dve.tensor_tensor(prob[:], L[:], hi[:].unsqueeze(2).to_broadcast(cols), ALU.subtract))
            dve.sem_inc(summed, 1)
            dve.wait_ge(exped, 1)
            st.link(dve.tensor_reduce(total[:], prob[:], AX.X, ALU.add))
            dve.sem_inc(esum, 1)
            dve.wait_ge(spread, 2)
            st.link(dve.reciprocal(total[:], pB[:, 0:NX]))
            st.link(dve.tensor_tensor(prob[:], prob[:], total[:].unsqueeze(2).to_broadcast(cols), ALU.mult))
            with dve.Fori(0, BIS // BU) as i:
                st.enter(i, 7 * BU)
                for j in range(BU):
                    st.link(dve.tensor_tensor(both[:], lo[:], hi[:], ALU.add))
                    at = st.value()
                    st.mark(dve.tensor_tensor(cmp[:], L2[:], both[:].unsqueeze(2).to_broadcast(cols), ALU.is_gt))
                    st.mark(dve.tensor_scalar(mid[:], both[:], 0.5, None, ALU.mult))
                    dve.wait_ge(step, at + 1)
                    with nc.allow_low_precision(reason="counts up to NT are exact in bfloat16"):
                        dve.tensor_reduce(cnt_b[:], cmp[:], AX.X, ALU.add).then_inc(counted, 1)
                    dve.wait_ge(totalled, i * BU + (j + 1))
                    st.mark(dve.tensor_scalar(more[:], pC[:], float(CAP), None, ALU.is_ge))
                    st.mark(dve.tensor_scalar(less[:], pC[:], float(CAP), None, ALU.is_lt))
                    wait_apart(dve, g, step, st.value())
                    st.mark(dve.copy_predicated(lo[:], more[:], mid[:]))
                    st.link(dve.copy_predicated(hi[:], less[:], mid[:]))
            st.leave(BIS // BU)
            st.mark(dve.tensor_tensor(gt[:], L[:], hi[:].unsqueeze(2).to_broadcast(cols), ALU.is_gt))
            st.link(dve.tensor_tensor(ge[:], L[:], lo[:].unsqueeze(2).to_broadcast(cols), ALU.is_gt))
            st.link(dve.tensor_tensor(ge[:], ge[:], gt[:], ALU.subtract))
            dve.sem_inc(picked, 1)
            for u, (m, place) in enumerate(((gt, pa), (ge, pb_))):
                dve.wait_ge(prefixed, u + 1)
                flat = lambda v: v[:].rearrange("p e t -> p (e t)")
                st.link(dve.tensor_tensor_scan(flat(tot), all_[u].rearrange("p e t -> p (e t)"), zz[:], 0.0,
                                               ALU.add, ALU.add))
                st.mark(dve.memset(start[:, u, 0:1], 0.0))
                st.mark(dve.tensor_copy(start[:, u, 1:NX], tot[:, 0:NX - 1, NT - 1]))
                if u == 0:
                    st.mark(dve.tensor_copy(cnt[:], tot[:, :, NT - 1]))
                st.link(dve.tensor_tensor(place[:], tot[:], all_[u], ALU.subtract))
                st.link(dve.tensor_tensor(place[:], place[:], pre[u], ALU.add))
                if u == 0:
                    st.link(dve.tensor_tensor(cnt[:], cnt[:], start[:, 0, :], ALU.subtract))
                else:
                    st.link(dve.tensor_tensor(start[:, 1, :], start[:, 1, :], cnt[:], ALU.subtract))
                st.link(dve.tensor_tensor(place[:], place[:], start[:, u, :].unsqueeze(2).to_broadcast(cols),
                                          ALU.subtract))
                st.link(dve.tensor_tensor(place[:], place[:], m[:], ALU.mult))
            st.mark(dve.tensor_tensor(pa[:], pa[:], pb_[:], ALU.add))
            st.link(dve.tensor_tensor(gt[:], gt[:], ge[:], ALU.add))
            st.link(dve.tensor_scalar(gt[:], gt[:], -9999.0, 9999.0, ALU.mult, ALU.add))
            st.link(dve.tensor_tensor(pa[:], pa[:], gt[:], ALU.add))
            st.link(dve.tensor_copy(digits[:, 0, :, :], pa[:]))
            st.link(dve.tensor_scalar(digits[:, 1, :, :], digits[:, 0, :, :], 7, None, ALU.logical_shift_right))
            st.link(dve.tensor_scalar(digits[:, 0, :, :], digits[:, 0, :, :], P - 1, None, ALU.bitwise_and))
            st.mark(dve.tensor_copy(lo_d[:], digits[:, 0, :, :]))
            st.link(dve.tensor_copy(hi_d[:], digits[:, 1, :, :]))
            dve.wait_ge(tok_ready, 2)
            for v in range(2):
                st.mark(dve.tensor_copy(part[:, :, :, v], tok[:, v, :].unsqueeze(1).to_broadcast(cols)))
            for v in range(2, 5):
                st.link(dve.tensor_copy(part[:, :, :, v], prob[:]))
                if v < 4:
                    st.link(dve.tensor_tensor(prob[:], prob[:], part[:, :, :, v], ALU.subtract))
            for c in range(NC):
                st.link(dve.tensor_scalar(match[:], hi_d[:], float(c), None, ALU.is_equal))
                st.link(dve.tensor_tensor(R[:, :, :, c, :].rearrange("p e t v -> p (e t) v"),
                                          part[:].rearrange("p e t v -> p (e t) v"),
                                          match[:].rearrange("p e t -> p (e t)").unsqueeze(2).to_broadcast(
                                              [P, NX * NT, 5]), ALU.mult))

            def batch(i, j):
                k = lo_d[:].rearrange("p e t -> p (e t)")[:, bass.ds(i * (2 * NT) + j * TB, TB)]
                dve.tensor_tensor(hotb[j % 2][:], iota_b[:].unsqueeze(1).to_broadcast([P, TB, P]),
                                  k.unsqueeze(2).to_broadcast([P, TB, P]), ALU.is_equal).then_inc(hot, 1)

            def unload(i, x):
                dve.wait_ge(packed, i * (2 * NB) + (x * NB + NB))
                col = i * (2 * NC) + x * NC
                f = lists_f[x]
                st.link(dve.tensor_copy(f[:].rearrange("p c v -> p (c v)"), pK[x]))
                dve.sem_inc(listed, 1)
                st.mark(dve.scalar_tensor_tensor(out=g.tok_i[:, bass.ds(col, NC)], in0=f[:, :, 0], scalar=float(P),
                                                 in1=f[:, :, 1], op0=ALU.mult, op1=ALU.add))
                st.link(dve.tensor_tensor(f[:, :, 3], f[:, :, 3], f[:, :, 4], ALU.add))
                st.link(dve.tensor_tensor(g.tok_p[:, bass.ds(col, NC)], f[:, :, 2], f[:, :, 3], ALU.add))

            def lists(i, first_lap):
                for j in range(2 * NB):
                    if not first_lap or j >= 2:
                        dve.wait_ge(packed, i * (2 * NB) + (j - 1))
                    batch(i, j)
                    if j == NB + 1:
                        unload(i, 0)
                    if j == 1 and not first_lap:
                        unload(i - 1, 1)

            lists(0, True)
            with dve.Fori(1, NX // 2) as i:
                st.enter(i - 1, 8)
                lists(i, False)
            st.leave(NX // 2 - 1)
            unload(NX // 2 - 1, 1)


def experts(nc, g):
    NC = CAP // P
    with ExitStack() as ctx:
        sb, sem, ps = g.maker(ctx)
        w_in, x_in, added = [sem(f"f_w{u}") for u in range(2)], g.sw["x_in"], g.sw["added"][0]
        staged, y_free, w_free, x_turned, x_copied, h_ready, h_done, y_ready, y_done, step = (sem(f"f_{n}") for n in (
            "staged", "y_free", "w_free", "xt", "xc", "h", "hd", "y", "yd", "step"))
        w1, w2, b1, b2 = ([sb(f"f{n}{u}", s) for u in range(2)] for n, s in (
            ("w1", [P, 4, FX]), ("w2", [P, 2, D]), ("b1", [P, 2]), ("b2", [P, D])))
        o = 0

        def arena(n):
            nonlocal o
            o += n
            return g.acc[:, o - n:o]

        X = [arena(NC * D).rearrange("p (c n) -> p c n", c=NC) for u in range(2)]
        Y = [arena(NC * D).rearrange("p (c n) -> p c n", c=NC) for u in range(2)]
        XT = arena(4 * CAP).rearrange("p (c n) -> p c n", c=4)
        HT = arena(2 * CAP).rearrange("p (c n) -> p c n", c=2)
        st_i = [sb(f"fi{u}", [P, NC], I32) for u in range(2)]
        pT = [ps(f"fT{u}", [P, CAP]) for u in range(2)]
        pH = [ps(f"fH{u}", [P, CAP]) for u in range(2)]
        pY = [ps(f"fY{u}", [P, D]) for u in range(2)]
        block = ctx.enter_context(nc.Block())

        @block.sync
        def _(sp):
            with sp.Fori(0, NX // 2) as i:
                for u in range(2):
                    e = i * 2 + u
                    sp.wait_ge(w_free, 2 * i + (u + 1))
                    sp.dma_start(w1[u][:], g.eW1[bass.ds(e * D, D), :].rearrange("(c p) n -> p c n", p=P))\
                      .then_inc(w_in[u], 16)
                    sp.dma_start(w2[u][:], g.eW2[bass.ds(e * FX, FX), :].rearrange("(c p) n -> p c n", p=P))\
                      .then_inc(w_in[u], 16)
                    sp.dma_start(b1[u][:], g.eb1[bass.ds(e * P, P), :]).then_inc(w_in[u], 16)
                    sp.dma_start(b2[u][:], g.eb2[bass.ds(e, 1), :].to_broadcast([P, D])).then_inc(w_in[u], 16)

        @block.gpsimd
        def _(pool):
            def gather(i, u):
                pool.tensor_copy(st_i[u][:], g.tok_i[:, bass.ds((2 * i + u) * NC, NC)]).then_inc(staged, 1)
                wait_apart(pool, g, staged, 2 * i + (u + 1))
                for c in range(NC):
                    pool.indirect_dma_start(X[u][:, c, :], None, g.q,
                                            bass.IndirectOffsetOnAxis(ap=st_i[u][:, c:c + 1], axis=0))\
                        .then_inc(x_in[u], 16)

            def scatter(i, u):
                wait_apart(pool, g, y_done, (2 * i + u) * NC + (NC + 1))
                for c in range(NC):
                    pool.indirect_dma_start(g.out, bass.IndirectOffsetOnAxis(ap=st_i[u][:, c:c + 1], axis=0),
                                            Y[u][:, c, :], None, compute_op=ALU.add).then_inc(added, 16)
                pool.wait_ge(added, (2 * i + (u + 1)) * (16 * NC))
                pool.sem_inc(y_free, 1)

            pool.sem_inc(y_free, 2)
            gather(0, 0)
            with pool.Fori(0, NX // 2 - 1) as i:
                gather(i, 1)
                scatter(i, 0)
                gather(i + 1, 0)
                scatter(i, 1)
            gather(NX // 2 - 1, 1)
            scatter(NX // 2 - 1, 0)
            scatter(NX // 2 - 1, 1)

        @block.tensor
        def _(pe):
            with pe.Fori(0, NX // 2) as i:
                for u in range(2):
                    e = 2 * i + u
                    pe.wait_ge(x_in[u], (16 * NC) * i + 16 * NC)
                    for c in range(4):
                        if c >= 2:
                            pe.wait_ge(x_copied, e * 4 + (c - 1))
                        for t in range(NC):
                            last = pe.transpose(pT[c % 2][:, t * P:(t + 1) * P], X[u][:, t, c * P:(c + 1) * P], g.ident[:])
                        last.then_inc(x_turned, 1)
                    pe.wait_ge(x_copied, e * 4 + 4)
                    pe.wait_ge(w_in[u], 64 * i + 64)
                    for f in range(2):
                        for c in range(4):
                            last = pe.matmul(pH[f][:], w1[u][:, c, f * P:(f + 1) * P], XT[:, c, :],
                                             start=(c == 0), stop=(c == 3))
                        last.then_inc(h_ready, 1)
                    pe.wait_ge(h_done, 2 * e + 2)
                    for t in range(NC):
                        pe.wait_ge(y_done, e * NC + (max(t - 1, 0) + 1))
                        for f in range(2):
                            last = pe.matmul(pY[t % 2][:], HT[:, f, t * P:(t + 1) * P], w2[u][:, f, :],
                                             start=(f == 0), stop=(f == 1))
                        last.then_inc(y_ready, 1)

        @block.scalar
        def _(act):
            with act.Fori(0, NX // 2) as i:
                for u in range(2):
                    e = 2 * i + u
                    for c in range(4):
                        act.wait_ge(x_turned, e * 4 + (c + 1))
                        act.activation(XT[:, c, :], pT[c % 2][:], ACT.Copy).then_inc(x_copied, 1)
                    act.wait_ge(w_in[u], 64 * i + 64)
                    for f in range(2):
                        act.wait_ge(h_ready, e * 2 + (f + 1))
                        act.activation(HT[:, f, :], pH[f][:], ACT.Gelu, bias=b1[u][:, f:f + 1]).then_inc(h_done, 1)

        @block.vector
        def _(dve):
            dve.sem_inc(w_free, 2)
            dve.sem_inc(y_done, 1)
            with dve.Fori(0, NX // 2) as i:
                for u in range(2):
                    e = 2 * i + u
                    dve.wait_ge(w_in[u], 64 * i + 64)
                    dve.wait_ge(y_free, 2 * i + (u + 1))
                    for t in range(NC):
                        dve.wait_ge(y_ready, e * NC + (t + 1))
                        y = Y[u][:, t, :]
                        dve.tensor_tensor(y, pY[t % 2][:], b2[u][:], ALU.add).then_inc(step, 1)
                        dve.wait_ge(step, e * NC + (t + 1))
                        dve.tensor_scalar(y, y, g.tok_p[:, bass.ds(e * NC + t, 1)], None, ALU.mult).then_inc(y_done, 1)
                    dve.wait_ge(y_done, e * NC + (NC + 1))
                    dve.sem_inc(w_free, 1)


class Shared:
    pass


def build(nc, x, src, dst, W_src, b_src, W_dst, b_dst, W_val, b_val, attn_l, attn_r, fc1T, fc1_b, fc2T, fc2_b,
          eps, gW1T, gb1, gW2T, gb2, gamma, beta, Wr, eW1, eb1, eW2, eb2, interp, out):
    g = Shared()
    row = lambda v: v.unsqueeze(0)
    g.x, g.src, g.dst, g.W_src, g.W_dst, g.W_val, g.fc1T, g.fc2T_d = x, src, dst, W_src, W_dst, W_val, fc1T, fc2T
    g.b_src, g.b_dst, g.b_val, g.attn_l, g.attn_r = row(b_src), row(b_dst), row(b_val), row(attn_l), row(attn_r)
    g.fc1_b, g.fc2_b, g.eps = fc1_b, row(fc2_b), row(eps)
    g.gW1T, g.gb1, g.gW2T, g.gb2, g.gamma, g.beta, g.Wr = gW1T, gb1, gW2T, row(gb2), row(gamma), row(beta), Wr
    g.eW1, g.eb1, g.eW2, g.eb2, g.interp, g.out = eW1, eb1, eW2, eb2, interp, out

    def dram(name, shape, dt=F32):
        return nc.dram_tensor(name, shape, dt, kind="Internal").ap()

    g.by_src = dram("by_src", [WL * PAIR, 2], I32)
    g.tiles_d = dram("tiles_d", [2, WL], I32)
    g.ve, g.x2, g.z, g.q = dram("ve", [NP, W]), dram("x2_d", [NP, D]), dram("z_d", [NP, D]), dram("q_d", [NP, D])

    with ExitStack() as ctx:
        def maker(c):
            sems = []

            def clear():
                if sems:
                    for n in sems:
                        nc.gpsimd.sem_clear(n)
                    nc.all_engine_barrier()

            c.callback(clear)

            def sb(name, shape, dt=F32):
                return c.enter_context(nc.sbuf_tensor(name, shape, dt))

            def sem(name):
                sems.append(c.enter_context(nc.semaphore(name)))
                return sems[-1]

            def ps(name, shape):
                n = int(np.prod(shape[1:]))
                t = c.enter_context(nc.psum_tensor(name, [shape[0], 512], F32))
                v = t[:][:, 0:n]
                if len(shape) > 2:
                    names = "abc"[:len(shape) - 1]
                    v = v.rearrange(f"p ({' '.join(names)}) -> p {' '.join(names)}",
                                    **{m: k for m, k in zip(names, shape[1:])})
                return v
            return sb, sem, ps

        g.maker = maker
        sb, new_sem, _ = maker(ctx)
        g.passed = new_sem("passed")
        g.sw = {n: [new_sem(f"sw_{n}{u}") for u in range(k)] for n, k in (
            ("rows", 1), ("scattered", 2), ("got0", 4 * QI), ("got1", 4 * QI), ("x_in", 2), ("added", 1))}
        g.acc = sb("acc", [P, NT * W])[:]
        g.ident, g.ones, g.upper, g.unpair, g.iota = (sb(n, [P, P]) for n in (
            "ident", "ones", "upper", "unpair", "iota"))
        g.pairup = sb("pairup", [P, P // 2])
        g.Wv, g.Wlr, g.bv, g.blr = sb("Wv", [P, 4, D]), sb("Wlr", [P, 4, 2 * H]), sb("bv", [P, D]), sb("blr", [P, 2 * H])
        g.Wf, g.fc1b, g.fc2T, g.fc2b = sb("Wf", [P, 2, HID]), sb("fc1b", [P, 2]), sb("fc2T", [P, 2, HID]), sb("fc2b", [1, HID])
        g.epsb, g.ln_eps = sb("epsb", [P, 1]), sb("ln_eps", [P, 1])
        g.erm = sb("erm", [P, NT * 2 * H])
        g.tile_base = sb("tile_base", [P, 2, 4])
        g.tiles = sb("tiles", [1, 2 * WL], I32)
        g.idx, g.key = sb("idx", [P, 2 * WL], I32), sb("key", [P, 2 * WL])
        g.tok_i, g.tok_p = sb("tok_i", [P, NX * 4], I32), sb("tok_p", [P, NX * 4])
        fold_consts(nc, g)
        with ExitStack() as early:
            esb, esem, _ = maker(early)
            g.rec, g.place = esb("rec", [P, EC, 2], I32), esb("place", [P, EC], I32)
            room = max(c for n, c in SCAT)
            g.place_st = [esb(f"place_st{u}", [P, room], I32) for u in range(2)]
            g.rec_st = [esb(f"rec_st{u}", [P, room, 2], I32) for u in range(2)]
            g.sc_staged = esem("sc_staged")
            with ExitStack() as plan:
                psb, _, _ = maker(plan)
                g.rows = psb("rows", [P, 4, 2, PAIR], I32)
                g.bucket_base, g.tiota = psb("bucket_base", [P, T]), psb("tiota", [P, T])
                plan_edges(nc, g)
                build_index(nc, g, 0)
                project(nc, g)
            edge_pass(nc, g, 0)
            wavelet_ffn(nc, g)
        with ExitStack() as mid:
            g.rows = maker(mid)[0]("rows1", [P, 4, 2, PAIR], I32)
            build_index(nc, g, 1)
        edge_pass(nc, g, 1)
        g.lg = sb("lg", [P, NX, NT])
        gin_mlp(nc, g)
        choose_tokens(nc, g)
        experts(nc, g)


def interpolation():
    n, m = D // 2, D
    pos = np.linspace(0.0, 1.0, m, dtype=np.float32) * np.float32(n - 1)
    i0 = np.clip(np.floor(pos).astype(np.int32), 0, n - 2)
    w = pos - i0.astype(np.float32)
    u = np.zeros((n, m), np.float32)
    u[i0, np.arange(m)] = np.float32(1.0) - w
    u[i0 + 1, np.arange(m)] += w
    return u


def layout(a):
    c = np.ascontiguousarray
    a = {k: np.asarray(v) for k, v in a.items()}
    pad = np.full(EP - NE, PAD_NODE, np.int32)
    m = {
        "x": np.concatenate([a["x"], np.zeros((NP - N, D), np.float32)]),
        "src": np.concatenate([a["src"], pad]), "dst": np.concatenate([a["dst"], pad]),
        "W_src": a["L0_gnn_W_src"], "b_src": a["L0_gnn_b_src"], "W_dst": a["L0_gnn_W_dst"],
        "b_dst": a["L0_gnn_b_dst"], "W_val": a["L0_gnn_W_val"], "b_val": a["L0_gnn_b_val"],
        "attn_l": a["L0_gnn_attn_l"].reshape(-1), "attn_r": a["L0_gnn_attn_r"].reshape(-1),
        "fc1T": a["L0_ffn_fc1_w"].T, "fc1_b": a["L0_ffn_fc1_b"].reshape(2, P).T, "fc2T": a["L0_ffn_fc2_w"].T,
        "fc2_b": a["L0_ffn_fc2_b"], "eps": a["L1_gnn_eps"].reshape(1), "gW1T": a["L1_gnn_W1"].T,
        "gb1": a["L1_gnn_b1"].reshape(4, P).T, "gW2T": a["L1_gnn_W2"].T, "gb2": a["L1_gnn_b2"], "gamma": a["L1_gnn_gamma"],
        "beta": a["L1_gnn_beta"], "Wr": a["L1_ffn_Wr"], "eW1": a["L1_ffn_W1"].reshape(NX * D, FX),
        "eb1": a["L1_ffn_b1"].reshape(NX, 2, P).transpose(0, 2, 1).reshape(NX * P, 2), "eW2": a["L1_ffn_W2"].reshape(NX * FX, D),
        "eb2": a["L1_ffn_b2"], "interp": c(interpolation().T),
    }
    return {k: c(v) for k, v in m.items()}


def kernel(**inputs):
    import concourse.bacc as bacc
    from concourse.bass_utils import run_bass_kernel_spmd

    arrays = layout(inputs)
    nc = bacc.Bacc("TRN2", target_bir_lowering=False, num_devices=1)
    aps = [nc.dram_tensor("in_" + k, v.shape, mybir.dt.from_np(v.dtype), kind="ExternalInput").ap()
           for k, v in arrays.items()]
    aps.append(nc.dram_tensor("out_nodes", (NP, D), F32, kind="ExternalOutput").ap())
    build(nc, *aps)
    r = run_bass_kernel_spmd(nc, [{"in_" + k: v for k, v in arrays.items()}], core_ids=[0])
    return r.results[0]["out_nodes"][:N]
```
